# Optimizing a Trainium2 kernel written in Bass

```python
import numpy as np
import jax
import jax.numpy as jnp

def _softmax(x, axis=-1):
    return jax.nn.softmax(x, axis=axis)

def _gelu(x):
    return jax.nn.gelu(x, approximate=True)

def _silu(x):
    return jax.nn.silu(x)

def _sigmoid(x):
    return jax.nn.sigmoid(x)

def _layernorm(x, axis=-1, eps=1e-05):
    m = jnp.mean(x, axis=axis, keepdims=True)
    v = jnp.var(x, axis=axis, keepdims=True)
    return (x - m) / jnp.sqrt(v + eps)

def _scatter_add(tgt, idx, src, axis=0):
    return tgt.at[idx].add(src)

def _segment_sum(src, seg, n):
    return jax.ops.segment_sum(src, seg, n)
kernel_name = 'mk_vit_tower_cls_d1_tok_img1024_r4_804c13'

def setup_inputs(seed: int=0):
    np.random.seed(seed)
    _w = jnp.asarray

    def _rec_inputs():
        import jax
        import jax.numpy as jnp
        _rk = jax.random.key(seed)
        x = -0.00150118 + 0.499729 * jax.random.normal(jax.random.fold_in(_rk, 1), (32, 256, 64, 2), jnp.float32)
        cls_tok = 0.02 * jax.random.normal(jax.random.fold_in(_rk, 5), (1, 1, 256), jnp.float32)
        return (x, cls_tok)
    x, cls_tok = _rec_inputs()

    def _L0_tok_setup():
        import jax, jax.numpy as jnp
        import numpy as np
        import math
        H = 256
        N = 64
        CH = 1
        SEQ_L = 256
        key = jax.random.key(seed)
        k1, k2, k3, k4 = jax.random.split(key, 4)
        log_dt = jax.random.uniform(k1, (H,), dtype=jnp.float32, minval=math.log(0.001), maxval=math.log(0.1))
        inv_A_real = jnp.log(0.5 * jnp.ones((H, N), jnp.float32)) + 0.1 * jax.random.normal(k2, (H, N), dtype=jnp.float32)
        A_imag = jnp.broadcast_to(math.pi * jnp.arange(N, dtype=jnp.float32), (H, N)).copy()
        B_ri = jax.random.normal(k3, (H, N, 2), dtype=jnp.float32) * 0.5
        C_ri = jax.random.normal(k4, (CH, H, N, 2), dtype=jnp.float32) * 0.5
        return {'log_dt': log_dt, 'inv_A_real': inv_A_real, 'A_imag': A_imag, 'B_ri': B_ri, 'C_ri': C_ri, 'L': SEQ_L}
    _L0_tok_all = _L0_tok_setup()
    _L0_tok_in = {k: v for k, v in _L0_tok_all.items() if k in ('log_dt', 'inv_A_real', 'A_imag', 'B_ri')}
    del _L0_tok_all

    def _L0_attn_setup():
        import jax, jax.numpy as jnp
        import numpy as np
        B, S, DIM, H, DH = (2, 512, 256, 16, 64)
        INNER = H * DH

        def _rmsnorm(t, gamma, scale):
            normed = t * jax.lax.rsqrt(jnp.mean(t * t, axis=-1, keepdims=True) + 1e-08)
            return normed * scale * gamma
        key = jax.random.key(seed)
        ks = jax.random.split(key, 4)
        sd = 0.02
        return {'x': jax.random.normal(ks[0], (B, S, DIM), dtype=jnp.float32), 'ln_w': jnp.ones((DIM,), jnp.float32), 'ln_b': jnp.zeros((DIM,), jnp.float32), 'Wq': jax.random.normal(ks[1], (DIM, INNER), jnp.float32) * sd, 'Wkv': jax.random.normal(ks[2], (DIM, 2 * INNER), jnp.float32) * sd, 'q_gamma': jnp.ones((H, 1, DH), jnp.float32), 'k_gamma': jnp.ones((H, 1, DH), jnp.float32), 'Wo': jax.random.normal(ks[3], (INNER, DIM), jnp.float32) * sd}
    _L0_attn_all = _L0_attn_setup()
    _L0_attn_in = {k: v for k, v in _L0_attn_all.items() if k in ('ln_w', 'ln_b', 'Wq', 'Wkv', 'q_gamma', 'k_gamma', 'Wo')}
    del _L0_attn_all

    def _L0_ffn_setup():
        import jax, jax.numpy as jnp
        import numpy as np
        D_MODEL = 256
        M = 64
        INNER = 16
        key = jax.random.key(seed)
        ks = jax.random.split(key, 9)

        def init(k, shape, fan_in):
            bound = 1.0 / np.sqrt(fan_in)
            return jax.random.uniform(k, shape, jnp.float32, -bound, bound)
        x = jax.random.normal(ks[0], (16, 1024, D_MODEL), dtype=jnp.float32)
        Win = init(ks[1], (D_MODEL, M), D_MODEL)
        bin_ = init(ks[2], (M,), D_MODEL)
        W1 = init(ks[3], (M, INNER), 1)
        b1 = init(ks[4], (M, INNER), 1)
        W2 = init(ks[5], (M, INNER), INNER)
        b2 = init(ks[6], (M,), INNER)
        Wout = init(ks[7], (M, D_MODEL), M)
        bout = init(ks[8], (D_MODEL,), M)
        return {'x': x, 'Win': Win, 'bin_': bin_, 'W1': W1, 'b1': b1, 'W2': W2, 'b2': b2, 'Wout': Wout, 'bout': bout}
    _L0_ffn_all = _L0_ffn_setup()
    _L0_ffn_in = {k: v for k, v in _L0_ffn_all.items() if k in ('Win', 'bin_', 'W1', 'b1', 'W2', 'b2', 'Wout', 'bout')}
    del _L0_ffn_all
    return {'x': x, 'cls_tok': cls_tok, 'L0_tok_log_dt': _L0_tok_in['log_dt'], 'L0_tok_inv_A_real': _L0_tok_in['inv_A_real'], 'L0_tok_A_imag': _L0_tok_in['A_imag'], 'L0_tok_B_ri': _L0_tok_in['B_ri'], 'L0_attn_ln_w': _L0_attn_in['ln_w'], 'L0_attn_ln_b': _L0_attn_in['ln_b'], 'L0_attn_Wq': _L0_attn_in['Wq'], 'L0_attn_Wkv': _L0_attn_in['Wkv'], 'L0_attn_q_gamma': _L0_attn_in['q_gamma'], 'L0_attn_k_gamma': _L0_attn_in['k_gamma'], 'L0_attn_Wo': _L0_attn_in['Wo'], 'L0_ffn_Win': _L0_ffn_in['Win'], 'L0_ffn_bin_': _L0_ffn_in['bin_'], 'L0_ffn_W1': _L0_ffn_in['W1'], 'L0_ffn_b1': _L0_ffn_in['b1'], 'L0_ffn_W2': _L0_ffn_in['W2'], 'L0_ffn_b2': _L0_ffn_in['b2'], 'L0_ffn_Wout': _L0_ffn_in['Wout'], 'L0_ffn_bout': _L0_ffn_in['bout']}

def reference(x, cls_tok, L0_tok_log_dt, L0_tok_inv_A_real, L0_tok_A_imag, L0_tok_B_ri, L0_attn_ln_w, L0_attn_ln_b, L0_attn_Wq, L0_attn_Wkv, L0_attn_q_gamma, L0_attn_k_gamma, L0_attn_Wo, L0_ffn_Win, L0_ffn_bin_, L0_ffn_W1, L0_ffn_b1, L0_ffn_W2, L0_ffn_b2, L0_ffn_Wout, L0_ffn_bout):
    import jax
    import jax.numpy as jnp

    def _L0_tok_ref(log_dt, inv_A_real, A_imag, B_ri, C_ri, L):
        import jax, jax.numpy as jnp
        import numpy as np
        import math
        H = 256
        N = 64
        CH = 1
        SEQ_L = 256
        dt = jnp.exp(log_dt)
        A = -jnp.exp(inv_A_real) + 1j * A_imag
        B = B_ri[..., 0] + 1j * B_ri[..., 1]
        C = C_ri[..., 0] + 1j * C_ri[..., 1]
        dtA = A * dt[:, None]
        dA = (1.0 + dtA / 2) / (1.0 - dtA / 2)
        C_term = C * B[None]
        log_dA = jnp.log(dA)
        V = jnp.exp(log_dA[:, :, None] * jnp.arange(L))
        K = 2.0 * jnp.einsum('chn,hnl->chl', C_term, V).real
        return K.astype(jnp.float32)

    def _L0_attn_ref(x, ln_w, ln_b, Wq, Wkv, q_gamma, k_gamma, Wo):
        import jax, jax.numpy as jnp
        import numpy as np
        B, S, DIM, H, DH = (2, 512, 256, 16, 64)
        INNER = H * DH

        def _rmsnorm(t, gamma, scale):
            normed = t * jax.lax.rsqrt(jnp.mean(t * t, axis=-1, keepdims=True) + 1e-08)
            return normed * scale * gamma
        h, dh = (q_gamma.shape[0], q_gamma.shape[-1])
        b, s, _ = x.shape
        mean = jnp.mean(x, axis=-1, keepdims=True)
        var = jnp.var(x, axis=-1, keepdims=True)
        xn = ln_w * (x - mean) / jnp.sqrt(var + 1e-05) + ln_b
        q = xn @ Wq
        k, v = jnp.split(xn @ Wkv, 2, axis=-1)
        to_heads = lambda t: t.reshape(b, s, h, dh).transpose(0, 2, 1, 3)
        q, k, v = (to_heads(q), to_heads(k), to_heads(v))
        scale = dh ** 0.5
        q = _rmsnorm(q, q_gamma, scale)
        k = _rmsnorm(k, k_gamma, scale)
        dots = jnp.einsum('bhid,bhjd->bhij', q, k)
        attn = jax.nn.softmax(dots, axis=-1)
        out = jnp.einsum('bhij,bhjd->bhid', attn, v)
        out = out.transpose(0, 2, 1, 3).reshape(b, s, h * dh)
        return out @ Wo

    def _L0_ffn_ref(x, Win, bin_, W1, b1, W2, b2, Wout, bout):
        import jax, jax.numpy as jnp
        import numpy as np
        D_MODEL = 256
        M = 64
        INNER = 16
        s = jnp.einsum('btd,dm->btm', x, Win) + bin_
        h = jax.nn.relu(s[..., None] * W1 + b1)
        g = jnp.einsum('btmh,mh->btm', h, W2) + b2
        out = jnp.einsum('btm,md->btd', g, Wout) + bout
        return out
    h = _L0_tok_ref(L0_tok_log_dt, L0_tok_inv_A_real, L0_tok_A_imag, L0_tok_B_ri, x, 256)
    h = jnp.concatenate([jnp.broadcast_to(cls_tok, (h.shape[0], 1, h.shape[2])), h], axis=1)
    h = h + _L0_attn_ref(_layernorm(h, axis=-1), L0_attn_ln_w, L0_attn_ln_b, L0_attn_Wq, L0_attn_Wkv, L0_attn_q_gamma, L0_attn_k_gamma, L0_attn_Wo)
    h = h + _L0_ffn_ref(_layernorm(h, axis=-1), L0_ffn_Win, L0_ffn_bin_, L0_ffn_W1, L0_ffn_b1, L0_ffn_W2, L0_ffn_b2, L0_ffn_Wout, L0_ffn_bout)
    return h

_drawn_inputs = setup_inputs


def setup_inputs(seed=0):
    import zlib

    import numpy as np

    out = dict(_drawn_inputs(seed))
    spreads = {'L0_attn_ln_w': (1.0, 0.2),
     'L0_attn_ln_b': (0.0, 0.277),
     'L0_attn_q_gamma': (1.0, 0.2),
     'L0_attn_k_gamma': (1.0, 0.2)}
    factors = {'cls_tok': 100.006,
     'L0_ffn_Win': 3.648,
     'L0_ffn_bin_': 8.0,
     'L0_ffn_W1': 3.566,
     'L0_ffn_bout': 3.434,
     'L0_ffn_b2': 2.714}
    for name, (base, spread) in spreads.items():
        noise = np.random.default_rng([zlib.crc32(name.encode()), seed]).standard_normal(out[name].shape)
        drawn = base * np.exp(spread * noise) if base else spread * noise
        out[name] = jnp.asarray(drawn.astype(out[name].dtype))
    for name, factor in factors.items():
        out[name] = (out[name] * factor).astype(out[name].dtype)
    return out
```

```python
from contextlib import ExitStack

import concourse.bass as bass
from concourse import mybir

F32 = mybir.dt.float32
ALU = mybir.AluOpType
ACT = mybir.ActivationFunctionType
AX = mybir.AxisListType

BATCHES = 32
P = 128
SEQ = 256
DIM = 256
NST = 64
HEADS, DH = 16, 64
INNER = HEADS * DH
TT = SEQ // P
LC = DIM // P
PAIRS = INNER // P
GROUPS = 4
M, MI = 64, 16
LN_EPS = 1e-5
RMS_EPS = 1e-8
HALVES = 4
STEP = DIM // HALVES
NC = 32
CHUNK = 16
QC, KC, VC, UC = 0, INNER, 2 * INNER, 3 * INNER
WCOLS = 3 * INNER + 2 * HEADS


class At:

    def __init__(self, add, reg=None, mul=0):
        self.add, self.reg, self.mul = add, reg, mul

    def __add__(self, n):
        return At(self.add + n, self.reg, self.mul)

    @property
    def parity(self):
        return self.add % 2

    @property
    def half(self):
        return At(self.add // 2, self.reg, self.mul // 2)

    def times(self, k):
        return self.add * k if self.reg is None else self.reg * (self.mul * k) + self.add * k


def wait(eng, sem, b, per, n):
    const = b.add * per + n
    if b.reg is None:
        if const > 0:
            eng.wait_ge(sem, const)
    else:
        assert const > 0
        eng.wait_ge(sem, b.reg * (b.mul * per) + const)


class Steps:

    def __init__(self, eng, sem, per):
        self.eng, self.sem, self.per, self.b, self.n = eng, sem, per, At(0), 0

    def begin(self, b):
        self.b, self.n = b, 0

    def did(self, ins):
        self.n += 1
        ins.then_inc(self.sem, 1)

    def settle(self):
        wait(self.eng, self.sem, self.b, self.per, self.n)

    def end(self):
        assert self.n == self.per, (self.n, self.per)



def token_program(nc, psum, ident, x, log_dt, inv_a, a_imag, b_ri, tokens):
    chunks = P // CHUNK
    ctx = ExitStack()
    with ctx:
        def sb(name, shape):
            return ctx.enter_context(nc.sbuf_tensor(name, shape, F32))

        def sem(name):
            return ctx.enter_context(nc.semaphore(name))

        dt_in = sb("dt_in", [P, 2])
        dt = sb("dt", [P, 2])
        e_const = sb("e_const", [P, 2])
        are = sb("are", [P, 2, NST])
        aim = sb("aim", [P, 2, NST])
        bri = sb("bri", [P, 2, NST, 2])
        nat = sb("nat", [P, 4, P])
        half_re = sb("half_re", [P, 2, NST])
        half_im = sb("half_im", [P, 2, NST])
        t0 = sb("t0", [P, P])
        t1 = sb("t1", [P, P])
        t2 = sb("t2", [P, P])
        xc = [sb(f"xc{i}", [P, 8, 2 * 2 * NST]) for i in range(2)]
        ct = sb("ct", [P, 2, P, NC])
        pw = sb("pw", [P, 6, 2, P])
        big = sb("big", [P, 3, 2, P])
        bp = sb("bp", [P, 4, P, HALVES])
        prod = [sb(f"prod{i}", [P, CHUNK * HALVES * NC]) for i in range(2)]
        cp = [sb(f"cp{i}", [P, 2, CHUNK, HALVES * NC]) for i in range(2)]
        qp = [sb(f"qp{i}", [P, 2, CHUNK, STEP]) for i in range(2)]
        qt = [sb(f"qt{i}", [P, CHUNK * STEP // 2]) for i in range(2)]
        qd = sb("qd", [P, 12, CHUNK])
        ko = [sb(f"ko{i}", [P, 8, STEP]) for i in range(4)]

        params_in = sem("params_in")
        c_in = [sem(f"c_in{i}") for i in range(4)]
        dt_ready = sem("dt_ready")
        exp_ready = sem("exp_ready")
        nat_ready = sem("nat_ready")
        nat_t = sem("nat_t")
        c_t = sem("c_t")
        c_copied = sem("c_copied")
        powers_ready = sem("powers_ready")
        dve_step = sem("tok_dve_step")
        pool_step = sem("tok_pool_step")
        cp_ready = sem("cp_ready")
        qp_ready = sem("qp_ready")
        mm_done = sem("mm_done")
        cp_re_ready = sem("cp_re_ready")
        ko_ready = sem("ko_ready")
        stored = [sem(f"stored{i}") for i in range(4)]
        block = ctx.enter_context(nc.Block())
        jobs = 4

        @block.sync
        def _(sp):
            for g in range(2):
                sp.dma_start(dt_in[:, g:g + 1], log_dt[g * P:(g + 1) * P].unsqueeze(1)).then_inc(params_in, 16)
            sp.dma_start(are[:, :, :], inv_a.rearrange("(g p) n -> p g n", g=2)).then_inc(params_in, 16)
            sp.dma_start(aim[:, :, :], a_imag.rearrange("(g p) n -> p g n", g=2)).then_inc(params_in, 16)
            sp.dma_start(bri[:, :, :, :], b_ri.rearrange("(g p) n r -> p g n r", g=2)).then_inc(params_in, 16)
            for i in range(4):
                cs = slice(i * 8, i * 8 + 8)
                if i >= 2:
                    sp.wait_ge(c_t, 16 * (i - 1))
                for g in range(2):
                    sp.dma_start(xc[i % 2][:, :, g * P:(g + 1) * P],
                                 x[cs, g * P:(g + 1) * P].rearrange("c p n r -> p c (n r)")).then_inc(c_in[i], 16)
            with sp.Fori(0, chunks) as k:
                for j in range(jobs):
                    sp.wait_ge(ko_ready, k * jobs + (j + 1))
                    g, half = j // 2, j % 2
                    for a in range(HALVES):
                        dst = tokens[:, bass.ds(k * CHUNK + (g * P + half * 8), 8), a * STEP:(a + 1) * STEP]
                        sp.dma_start(dst, ko[j][a * NC:(a + 1) * NC, :, :]).then_inc(stored[j], 16)
            for j in range(4):
                sp.wait_ge(stored[j], 16 * HALVES * chunks)

        @block.scalar
        def _(act):
            act.wait_ge(params_in, 80)
            nc.scalar.activation(half_re[:, :, :], are[:, :, :], ACT.Exp).then_inc(exp_ready, 1)
            for j in range(16):
                r, c0 = j % 2, 4 * (j // 2)
                act.wait_ge(c_t, 4 * j + 4)
                nc.scalar.activation(ct[:, r, :, c0:c0 + 4],
                                     psum[1 + j % 2][:, :].rearrange("p (c h) -> p h c", c=4),
                                     ACT.Copy).then_inc(c_copied, 1)
            def features_out(k):
                for j in range(jobs):
                    wait(act, mm_done, k, jobs, j + 1)
                    wait(act, stored[j], k, 16 * HALVES, 0)
                    nc.scalar.activation(ko[j][:, :, :],
                                         psum[3 + j][:, :].rearrange("p (h b) -> p h b", h=8),
                                         ACT.Copy).then_inc(ko_ready, 1)

            features_out(At(0))
            with act.Fori(0, chunks - 1) as k:
                features_out(At(1, k, 1))

        @block.tensor
        def _(pe):
            pe.wait_ge(nat_ready, 1)
            for i in range(4):
                nc.tensor.transpose(psum[0][:, i * P:(i + 1) * P], nat[:, i, :], ident[:, :]).then_inc(nat_t, 1)
            for j in range(16):
                r, c0 = j % 2, 4 * (j // 2)
                if j % 4 == 0:
                    pe.wait_ge(c_in[j // 4], 32)
                if j >= 2:
                    pe.wait_ge(c_copied, j - 1)
                for c in range(4):
                    nc.tensor.transpose(psum[1 + j % 2][:, c * P:(c + 1) * P],
                                        xc[j // 4 % 2][:, (c0 + c) % 8, r::2], ident[:, :]).then_inc(c_t, 1)

            def product(k):
                par = k.parity
                wait(pe, cp_ready, k, 1, 1)
                wait(pe, qp_ready, k, 1, 1)
                for j in range(jobs):
                    g, half = j // 2, j % 2
                    rows = slice(g * NST, (g + 1) * NST)
                    wait(pe, ko_ready, k, jobs, j + 1 - jobs)
                    for h in range(8):
                        for r in range(2):
                            last = nc.tensor.matmul(psum[3 + j][:, h * STEP:(h + 1) * STEP],
                                                    cp[par][rows, r, half * 8 + h, :],
                                                    qp[par][rows, r, half * 8 + h, :],
                                                    start=(r == 0), stop=(r == 1))
                    last.then_inc(mm_done, 1)

            product(At(0))
            product(At(1))
            with pe.Fori(0, chunks // 2 - 1) as k2:
                product(At(2, k2, 2))
                product(At(3, k2, 2))

        @block.vector
        def _(dve):
            count = [0]

            def link(ins):
                count[0] += 1
                ins.then_inc(dve_step, 1)
                dve.wait_ge(dve_step, count[0])

            def tt(out, a, b, op):
                return nc.vector.tensor_tensor(out, a, b, op)

            def cmul(o, a, b, u, v, final=None):
                link(tt(u, a[0], b[0], ALU.mult))
                link(tt(v, a[1], b[1], ALU.mult))
                link(tt(o[0], u, v, ALU.subtract))
                link(tt(u, a[0], b[1], ALU.mult))
                link(tt(v, a[1], b[0], ALU.mult))
                if final is None:
                    link(tt(o[1], u, v, ALU.add))
                else:
                    tt(o[1], u, v, ALU.add).then_inc(final, 1)
                    dve.wait_ge(final, 1)

            dve.wait_ge(params_in, 80)
            dve.wait_ge(dt_ready, 1)
            dve.wait_ge(exp_ready, 1)
            dtb = dt[:, :].unsqueeze(2).to_broadcast([P, 2, NST])
            f = lambda t: t[:, :, :].rearrange("p g n -> p (g n)")
            link(tt(half_im[:, :, :], aim[:, :, :], dtb, ALU.mult))
            link(nc.vector.tensor_scalar(half_im[:, :, :], half_im[:, :, :], 0.5, None, ALU.mult))
            link(tt(half_re[:, :, :], half_re[:, :, :], dtb, ALU.mult))
            link(nc.vector.tensor_scalar(half_re[:, :, :], half_re[:, :, :], -0.5, None, ALU.mult))
            link(tt(t2[:, :], f(half_im), f(half_im), ALU.mult))
            link(nc.vector.tensor_scalar(t0[:, :], f(half_re), -1.0, 1.0, ALU.mult, ALU.add))
            link(tt(t1[:, :], t0[:, :], t0[:, :], ALU.mult))
            link(tt(t1[:, :], t1[:, :], t2[:, :], ALU.add))
            link(nc.vector.reciprocal(t1[:, :], t1[:, :]))
            link(nc.vector.scalar_tensor_tensor(t0[:, :], f(half_re), 1.0, t0[:, :], ALU.add, ALU.mult))
            link(tt(t0[:, :], t0[:, :], t2[:, :], ALU.subtract))
            link(tt(nat[:, 0, :], t0[:, :], t1[:, :], ALU.mult))
            link(nc.vector.scalar_tensor_tensor(nat[:, 1, :], f(half_im), 2.0, t1[:, :], ALU.mult, ALU.mult))
            bv = bri[:, :, :, :].rearrange("p g n r -> p r (g n)")
            link(nc.vector.tensor_copy(nat[:, 2, :], bv[:, 0, :]))
            nc.vector.tensor_copy(nat[:, 3, :], bv[:, 1, :]).then_inc(nat_ready, 1)
            dve.wait_ge(nat_t, 4)
            link(nc.vector.tensor_copy(pw[:, 0, :, :], psum[0][:, 0:2 * P].rearrange("p (r h) -> p r h", r=2)))
            bt = [t1[:, :], t2[:, :]]
            for r in range(2):
                link(nc.vector.tensor_scalar(bt[r], psum[0][:, (2 + r) * P:(3 + r) * P], 2.0, None, ALU.mult))
            u, v = t0[:, :], half_re[:, :, :].rearrange("p g n -> p (g n)")
            steps = [pw[:, i] for i in range(6)] + [big[:, 0], big[:, 1]]
            for i in range(1, 8):
                a = (steps[i - 1][:, 0, :], steps[i - 1][:, 1, :])
                cmul((steps[i][:, 0, :], steps[i][:, 1, :]), a, a, u, v, powers_ready if i == 5 else None)
            d64 = (big[:, 0, 0, :], big[:, 0, 1, :])
            d128 = (big[:, 1, 0, :], big[:, 1, 1, :])
            d192 = (big[:, 2, 0, :], big[:, 2, 1, :])
            cmul(d192, d64, d128, u, v)
            for r in range(2):
                link(nc.vector.tensor_copy(bp[:, r, :, 0], bt[r]))
            for a, d in ((1, d64), (2, d128), (3, d192)):
                cmul((bp[:, 0, :, a], bp[:, 1, :, a]), bt, d, u, v)
            link(nc.vector.tensor_scalar(bp[:, 2:4, :, :], bp[:, 0:2, :, :], -1.0, None, ALU.mult))
            done = count[0]
            dve.wait_ge(c_copied, 16)

            def stationary(k):
                par = k.parity
                hs = bass.ds(k.times(CHUNK), CHUNK)
                full = [P, CHUNK, HALVES, NC]
                c = [ct[:, r, hs, :].unsqueeze(2).to_broadcast(full) for r in range(2)]
                w = [bp[:, i, hs, :].unsqueeze(3).to_broadcast(full) for i in range(4)]
                pv = [t[:, :].rearrange("p (h a c) -> p h a c", h=CHUNK, a=HALVES) for t in prod]
                o = [cp[par][:, r, :, :].rearrange("p h (a c) -> p h a c", a=HALVES) for r in range(2)]
                wait(dve, mm_done, k, jobs, -jobs)
                tt(pv[0], c[0], w[0], ALU.mult).then_inc(dve_step, 1)
                tt(pv[1], c[1], w[1], ALU.mult).then_inc(dve_step, 1)
                wait(dve, dve_step, k, 4, done + 2)
                tt(o[0], pv[0], pv[1], ALU.subtract).then_inc(cp_re_ready, 1)
                wait(dve, cp_re_ready, k, 1, 1)
                tt(pv[0], c[0], w[3], ALU.mult).then_inc(dve_step, 1)
                tt(pv[1], c[1], w[2], ALU.mult).then_inc(dve_step, 1)
                wait(dve, dve_step, k, 4, done + 4)
                tt(o[1], pv[0], pv[1], ALU.add).then_inc(cp_ready, 1)
                wait(dve, cp_ready, k, 1, 1)

            stationary(At(0))
            stationary(At(1))
            with dve.Fori(0, chunks // 2 - 1) as k2:
                stationary(At(2, k2, 2))
                stationary(At(3, k2, 2))

        @block.gpsimd
        def _(pool):
            pool.memset(e_const[:, :], 2.718281828459045).then_inc(pool_step, 1)
            pool.wait_ge(params_in, 80)
            pool.wait_ge(pool_step, 1)
            pool.tensor_tensor(dt[:, :], e_const[:, :], dt_in[:, :], ALU.pow).then_inc(dt_ready, 1)
            for par in range(2):
                pool.memset(qp[par][:, 0, :, 0:1], 1.0).then_inc(pool_step, 1)
                pool.memset(qp[par][:, 1, :, 0:1], 0.0).then_inc(pool_step, 1)
            pool.wait_ge(pool_step, 5)
            pool.wait_ge(powers_ready, 1)
            first, per = 5, 2 + 5 * 6 - 1

            def moving(k):
                q = qp[k.parity]
                hs = bass.ds(k.times(CHUNK), CHUNK)
                wait(pool, mm_done, k, jobs, -jobs)
                pool.tensor_copy(qd[:, :, :], pw[:, :, :, hs].rearrange("p i r h -> p (i r) h")).then_inc(pool_step, 1)
                pool.tensor_copy(q[:, :, :, 1:2], pw[:, 0, :, hs].unsqueeze(3)).then_inc(pool_step, 1)
                n = 2
                wait(pool, pool_step, k, per, first + n)
                for i in range(1, 6):
                    m = 1 << i
                    d = [qd[:, 2 * i + r, :].unsqueeze(2).to_broadcast([P, CHUNK, m]) for r in range(2)]
                    s = [q[:, r, :, 0:m] for r in range(2)]
                    u = [t[:, 0:CHUNK * m].rearrange("p (h b) -> p h b", h=CHUNK) for t in qt]
                    pool.tensor_tensor(u[0], s[0], d[0], ALU.mult).then_inc(pool_step, 1)
                    pool.tensor_tensor(u[1], s[1], d[1], ALU.mult).then_inc(pool_step, 1)
                    wait(pool, pool_step, k, per, first + n + 2)
                    pool.tensor_tensor(q[:, 0, :, m:2 * m], u[0], u[1], ALU.subtract).then_inc(pool_step, 1)
                    wait(pool, pool_step, k, per, first + n + 3)
                    pool.tensor_tensor(u[0], s[0], d[1], ALU.mult).then_inc(pool_step, 1)
                    pool.tensor_tensor(u[1], s[1], d[0], ALU.mult).then_inc(pool_step, 1)
                    wait(pool, pool_step, k, per, first + n + 5)
                    last = pool.tensor_tensor(q[:, 1, :, m:2 * m], u[0], u[1], ALU.add)
                    if i < 5:
                        last.then_inc(pool_step, 1)
                        wait(pool, pool_step, k, per, first + n + 6)
                        n += 6
                    else:
                        last.then_inc(qp_ready, 1)
                        wait(pool, qp_ready, k, 1, 1)
                assert n + 5 == per, n

            moving(At(0))
            moving(At(1))
            with pool.Fori(0, chunks // 2 - 1) as k2:
                moving(At(2, k2, 2))
                moving(At(3, k2, 2))



class Weights:

    def __init__(self, nc, ctx):
        def sb(name, shape):
            return ctx.enter_context(nc.sbuf_tensor(name, shape, F32))

        self.w = sb("w", [P, LC, WCOLS])
        self.wo = sb("wo", [P, PAIRS, DIM])
        self.w_in = sb("w_in", [P, LC, 2 * M])
        self.w_out = sb("w_out", [P, TT, DIM])
        self.b_out = sb("b_out", [P, DIM])
        self.ln_w = sb("ln_w", [P, DIM])
        self.ln_b = sb("ln_b", [P, DIM])
        self.w1 = sb("w1", [P, MI])
        self.b1 = sb("b1", [P, MI])
        self.w2 = sb("w2", [P, MI])
        self.b_in = sb("b_in", [P, 1])
        self.b2 = sb("b2", [P, 1])
        self.cls = sb("cls", [P, DIM])
        self.v_cls = sb("v_cls", [P, INNER])
        self.gam = sb("gam", [P, PAIRS])
        self.z = sb("z_cls", [HEADS, DIM])
        self.scc = sb("scc", [HEADS, 1])
        self.half = sb("half", [P, 2 * HEADS])


def class_program(nc, psum, ident, wt, cls_tok, ln_w, ln_b, wq, wkv, q_gamma, k_gamma, wo,
                  w_in, b_in, w1, b1, w2, b2, w_out, b_out):
    ctx = ExitStack()
    with ctx:
        def sb(name, shape):
            return ctx.enter_context(nc.sbuf_tensor(name, shape, F32))

        def sem(name):
            return ctx.enter_context(nc.semaphore(name))

        stats = sb("c_stats", [P, 6])
        mv = sb("c_mv", [P, 2])
        rstd = sb("c_rstd", [P, 1])
        xn = sb("c_xn", [P, DIM])
        xnt = sb("c_xnt", [P, LC, P])
        gq = sb("c_gq", [P, INNER])
        gk = sb("c_gk", [P, INNER])
        row = [sb(f"c_row{i}", [P, INNER]) for i in range(2)]
        tmp = sb("c_tmp", [P, INNER])
        ss = sb("c_ss", [P, 2, HEADS])
        rr = sb("c_rr", [P, 2, HEADS])
        cc = sb("c_cc", [P, HEADS])
        vb = sb("c_vb", [P, PAIRS, HEADS])

        loaded = sem("loaded")
        var_ready = sem("c_var_ready")
        rstd_ready = sem("c_rstd_ready")
        pe_step = sem("c_pe_step")
        dve_step = sem("c_dve_step")
        pool_step = sem("c_pool_step")
        ss_ready = sem("c_ss_ready")
        rr_ready = sem("c_rr_ready")
        xn_ready = sem("c_xn_ready")
        xnt_ready = sem("c_xnt_ready")
        rows_ready = sem("c_rows_ready")
        cc_ready = sem("c_cc_ready")
        vb_ready = sem("c_vb_ready")
        block = ctx.enter_context(nc.Block())

        @block.sync
        def _(sp):
            n = 0

            def load(dst, src):
                nonlocal n
                n += 1
                sp.dma_start(dst, src).then_inc(loaded, 16)

            load(wt.cls[:, :], cls_tok[0, 0, :].partition_broadcast(P))
            load(wt.ln_w[:, :], ln_w.partition_broadcast(P))
            load(wt.ln_b[:, :], ln_b.partition_broadcast(P))
            load(wt.w[:, :, QC:QC + INNER], wq.rearrange("(c p) n -> p c n", p=P))
            load(wt.w[:, :, KC:KC + 2 * INNER], wkv.rearrange("(c p) n -> p c n", p=P))
            load(gq[:, :], q_gamma.rearrange("h o d -> (h o d)").partition_broadcast(P))
            load(gk[:, :], k_gamma.rearrange("h o d -> (h o d)").partition_broadcast(P))
            load(wt.wo[:, :, :], wo.rearrange("(c p) n -> p c n", p=P))
            load(wt.b_out[:, :], b_out.partition_broadcast(P))
            for i in range(2):
                rows = slice(i * M, (i + 1) * M)
                load(wt.w_in[:, :, rows], w_in.rearrange("(c p) m -> p c m", p=P))
                load(wt.w_out[rows, i, :], w_out)
                load(wt.w1[rows, :], w1)
                load(wt.b1[rows, :], b1)
                load(wt.w2[rows, :], w2)
                load(wt.b_in[rows, :], b_in.unsqueeze(1))
                load(wt.b2[rows, :], b2.unsqueeze(1))
            assert n == LOADS, n

        @block.gpsimd
        def _(pool):
            pool.memset(wt.half[:, :], -0.5).then_inc(pool_step, 1)
            pool.wait_ge(pool_step, 1)
            pool.wait_ge(var_ready, 1)
            pool.tensor_tensor(rstd[:, :], mv[:, 1:2], wt.half[:, 0:1], ALU.pow).then_inc(rstd_ready, 1)
            pool.wait_ge(ss_ready, 1)
            pool.tensor_tensor(rr[:, :, :].rearrange("p a h -> p (a h)"),
                               ss[:, :, :].rearrange("p a h -> p (a h)"), wt.half[:, :], ALU.pow).then_inc(rr_ready, 1)

        @block.tensor
        def _(pe):
            pe.wait_ge(xn_ready, 1)
            for c in range(LC):
                nc.tensor.transpose(psum[0][:, c * P:(c + 1) * P], xn[:, c * P:(c + 1) * P],
                                    ident[:, :]).then_inc(pe_step, 1)
            pe.wait_ge(xnt_ready, 1)
            for j in range(6):
                for c in range(LC):
                    last = nc.tensor.matmul(psum[1 + j][:, :], xnt[:, c, :], wt.w[:, c, j * 512:(j + 1) * 512],
                                            start=(c == 0), stop=(c == LC - 1))
                last.then_inc(pe_step, 1)
            pe.wait_ge(rows_ready, 1)
            for src, bank in ((wt.v_cls, (0, 7)), (tmp, (1, 2))):
                for c in range(PAIRS):
                    nc.tensor.transpose(psum[bank[c // 4]][:, (c % 4) * P:(c % 4 + 1) * P],
                                        src[:, c * P:(c + 1) * P], ident[:, :]).then_inc(pe_step, 1)
            pe.wait_ge(cc_ready, 1)
            nc.tensor.transpose(psum[3][0:HEADS, 0:P], cc[:, :], ident[:, :]).then_inc(pe_step, 1)
            pe.wait_ge(vb_ready, 1)
            for c in range(PAIRS):
                last = nc.tensor.matmul(psum[4][0:HEADS, 0:DIM], vb[:, c, :], wt.wo[:, c, :],
                                        start=(c == 0), stop=(c == PAIRS - 1))
            last.then_inc(pe_step, 1)

        @block.vector
        def _(dve):
            count = [0]

            def link(ins):
                count[0] += 1
                ins.then_inc(dve_step, 1)
                dve.wait_ge(dve_step, count[0])

            tt, ts = nc.vector.tensor_tensor, nc.vector.tensor_scalar
            for i in range(TT):
                link(nc.vector.memset(wt.w_out[(1 - i) * M:(2 - i) * M, i, :], 0.0))
            dve.wait_ge(loaded, 16 * LOADS)
            link(nc.vector.bn_stats(stats[:, :], wt.cls[:, :]))
            link(nc.vector.bn_aggr(mv[:, :], stats[:, :]))
            ts(mv[:, 1:2], mv[:, 1:2], 1.0 + LN_EPS, LN_EPS * LN_EPS, ALU.mult, ALU.add).then_inc(var_ready, 1)
            dve.wait_ge(rstd_ready, 1)
            link(ts(xn[:, :], wt.cls[:, :], mv[:, 0:1], rstd[:, 0:1], ALU.subtract, ALU.mult))
            link(tt(xn[:, :], xn[:, :], wt.ln_w[:, :], ALU.mult))
            tt(xn[:, :], xn[:, :], wt.ln_b[:, :], ALU.add).then_inc(xn_ready, 1)
            dve.wait_ge(pe_step, LC)
            nc.vector.tensor_copy(xnt[:, :, :].rearrange("p c t -> p (c t)"), psum[0][:, 0:LC * P]).then_inc(xnt_ready, 1)
            heads = lambda ap: ap.rearrange("p (h d) -> p h d", d=DH)
            for i in range(2):
                dve.wait_ge(pe_step, LC + 2 * i + 2)
                for j in range(2):
                    link(nc.vector.tensor_copy(row[i][:, j * 512:(j + 1) * 512], psum[1 + 2 * i + j][:, :]))
                link(tt(tmp[:, :], row[i][:, :], row[i][:, :], ALU.mult))
                link(nc.vector.tensor_reduce(ss[:, i, :], heads(tmp[:, :]), AX.X, ALU.add))
            ts(ss[:, :, :], ss[:, :, :], 1.0 / DH, RMS_EPS, ALU.mult, ALU.add).then_inc(ss_ready, 1)
            dve.wait_ge(pe_step, LC + 6)
            for j in range(2):
                link(nc.vector.tensor_copy(wt.v_cls[:, j * 512:(j + 1) * 512], psum[5 + j][:, :]))
            link(tt(tmp[:, :], gq[:, :], gk[:, :], ALU.mult))
            ts(tmp[:, :], tmp[:, :], float(DH), None, ALU.mult).then_inc(rows_ready, 1)
            dve.wait_ge(rows_ready, 1)
            dve.wait_ge(rr_ready, 1)
            rb = [rr[:, i, :].unsqueeze(2).to_broadcast([P, HEADS, DH]) for i in range(2)]
            link(tt(heads(row[1][:, :]), heads(row[1][:, :]), rb[1], ALU.mult))
            link(tt(heads(row[0][:, :]), heads(row[0][:, :]), rb[0], ALU.mult))
            link(tt(row[0][:, :], row[0][:, :], tmp[:, :], ALU.mult))
            link(tt(gq[:, :], row[0][:, :], row[1][:, :], ALU.mult))
            nc.vector.tensor_reduce(cc[:, :], heads(gq[:, :]), AX.X, ALU.add).then_inc(cc_ready, 1)
            link(tt(row[1][:, :], row[1][:, :], tmp[:, :], ALU.mult))
            dve.wait_ge(cc_ready, 1)
            for i, (base, r) in enumerate(((KC, row[0]), (QC, row[1]))):
                for c in range(LC):
                    link(tt(gq[:, :], wt.w[:, c, base:base + INNER], r[:, :], ALU.mult))
                    link(nc.vector.tensor_reduce(wt.w[:, c, UC + i * HEADS:UC + (i + 1) * HEADS],
                                                 heads(gq[:, :]), AX.X, ALU.add))
            link(nc.vector.memset(vb[:, :, :], 0.0))
            dve.wait_ge(pe_step, LC + 6 + 2 * PAIRS)
            flat = vb[:, :, :].rearrange("p c h -> p (c h)")
            for half in range(2):
                bank = psum[(0, 7)[half]][:, :].rearrange("p (c t) -> p c t", t=P)
                gbank = psum[(1, 2)[half]][:, :].rearrange("p (c t) -> p c t", t=P)
                link(nc.vector.tensor_copy(wt.gam[:, 4 * half:4 * half + 4], gbank[:, :, 0]))
                for i in range(2):
                    rows = slice(i * DH, (i + 1) * DH)
                    lo = 4 * half * (HEADS + 2) + i
                    last = nc.vector.tensor_copy(flat[rows, lo:lo + 3 * (HEADS + 2) + 1:HEADS + 2], bank[rows, :, 0])
                    if half and i:
                        last.then_inc(vb_ready, 1)
                    else:
                        link(last)
            dve.wait_ge(pe_step, LC + 6 + 2 * PAIRS + 1)
            link(nc.vector.tensor_copy(wt.scc[:, :], psum[3][0:HEADS, 0:1]))
            dve.wait_ge(pe_step, LC + 6 + 2 * PAIRS + 2)
            link(nc.vector.tensor_copy(wt.z[:, :], psum[4][0:HEADS, 0:DIM]))


LOADS = 9 + 2 * 7



FRONT = [("xt", 3, "dve"),
         ("k00", 3, "act"), ("k01", 4, "act"), ("k10", 5, "act"), ("k11", 6, "act"), ("u", 6, "dve"),
         ("q00", 7, "act"), ("q01", 8, "act"), ("q10", 9, "act"), ("q11", 10, "act"),
         ("lc", 11, "act"), ("v00", 11, "act"), ("kt0", 11, "dve"),
         ("v01", 12, "act"), ("kt1", 12, "dve"),
         ("v10", 13, "act"), ("kt2", 13, "dve"), ("qt0", 13, "act"), ("pc", 13, "dve"),
         ("v11", 14, "act"), ("kt3", 14, "dve"), ("qt1", 14, "act"),
         ("qt2", 15, "act"), ("qt3", 15, "act"), ("xb", 15, "dve")]
BACK = [("ot0", 0, "act"), ("ot1", 1, "act"), ("ot2", 2, "act"), ("ot3", 3, "act"), ("pt", 3, "dve"),
        ("wo", 4, "dve"), ("z2t", 8, "dve"), ("s", 9, "act"), ("y", 15, "dve")]
OT3_SLOT = 3


class Jobs:

    def __init__(self, table, banks, ready, freed):
        self.table, self.banks, self.ready, self.freed = table, banks, ready, freed
        self.at = {name: i for i, (name, _, _) in enumerate(table)}
        self.count = {e: sum(x[2] == e for x in table) for e in ("act", "dve")}

    def in_slot(self, slot, engine=None):
        return [n for n, s, e in self.table if s == slot and (engine is None or e == engine)]

    def bank(self, name):
        return self.banks[self.at[name] % len(self.banks)]

    def wait_ready(self, eng, b, name):
        wait(eng, self.ready, b, len(self.table), self.at[name] + 1)

    def wait_copied(self, eng, b, name):
        i = self.at[name]
        e = self.table[i][2]
        wait(eng, self.freed[e], b, self.count[e], sum(x[2] == e for x in self.table[:i + 1]))

    def wait_bank(self, eng, b, name):
        i = self.at[name] - len(self.banks)
        if len(self.table) % len(self.banks) and i < 0:
            for j in range(len(self.table) - len(self.banks), len(self.table)):
                self.wait_copied(eng, b + -1, self.table[j][0])
            return
        if i < 0:
            self.wait_copied(eng, b + -1, self.table[i][0])
        else:
            self.wait_copied(eng, b, self.table[i][0])


def image_program(nc, psum, ident, wt, tokens, xb, pcc, out):
    ctx = ExitStack()
    with ctx:
        def sb(name, shape):
            return ctx.enter_context(nc.sbuf_tensor("i_" + name, shape, F32))

        def two(name, shape):
            return [sb(f"{name}{i}", shape) for i in range(2)]

        def sem(name):
            return ctx.enter_context(nc.semaphore(name))

        x = two("x", [P, TT, DIM])
        carrier = sb("carrier", [P, 1])
        bn = sb("bn", [P, TT, 6])
        mv = sb("mv", [P, TT, 2])
        rstd = sb("rstd", [P, TT])
        zn = sb("zn", [P, TT, DIM])
        xn = two("xn", [P, TT, DIM])
        xnt = sb("xnt", [P, LC, SEQ])
        qs = sb("qs", [P, TT, INNER])
        ks = sb("ks", [P, TT, INNER])
        sq = two("sq", [P, 512])
        ss = sb("ss", [P, 2, TT, HEADS])
        rk = sb("rk", [P, TT, HEADS])
        rq = two("rq", [P, TT, HEADS])
        u = two("u", [P, TT, 2 * HEADS])
        v = two("v", [P, TT, INNER])
        qt = two("qt", [P, PAIRS, SEQ])
        kt = two("kt", [P, PAIRS, SEQ])
        lc = sb("lc", [P, TT, HEADS])
        cm = sb("cm", [HEADS, 1])
        ncm = sb("ncm", [HEADS, 1])
        ce = sb("ce", [HEADS, SEQ])
        cs = sb("cs", [HEADS, 1])
        cse = sb("cse", [HEADS, 1])
        csum = sb("csum", [HEADS, 1])
        cinv = sb("cinv", [HEADS, 1])
        cp = sb("cp", [HEADS, SEQ])
        cpt = sb("cpt", [P, TT, HEADS])
        nrq = sb("nrq", [P, TT, HEADS])
        ru = sb("ru", [P, TT, HEADS])
        mx = sb("mx", [P, TT])
        mxc = sb("mxc", [P, TT])
        nb = sb("nb", [P, TT, HEADS])
        e = two("e", [P, TT, SEQ])
        esum = sb("esum", [P, TT, HEADS])
        earg = sb("earg", [P, TT, HEADS])
        ecls = sb("ecls", [P, TT, HEADS])
        den = sb("den", [P, TT, 4])
        rinv = sb("rinv", [P, TT, HEADS])
        pt = two("pt", [P, TT, SEQ])
        o = sb("o", [P, TT, INNER])
        pcls = sb("pcls", [P, TT, HEADS])
        ot = sb("ot", [P, PAIRS, SEQ])
        pclst = sb("pclst", [HEADS, SEQ])
        xr = sb("xr", [P, TT, DIM])
        h1 = sb("h1", [P, TT, DIM])
        bn2 = sb("bn2", [P, TT, 6])
        mv2 = sb("mv2", [P, TT, 2])
        rstd2 = sb("rstd2", [P, TT])
        z2 = sb("z2", [P, TT, DIM])
        hb = sb("hb", [P, TT, DIM])
        yt = sb("yt", [P, LC, SEQ])
        st = sb("st", [P, P])
        relu = [sb(f"relu{i}", [P, P]) for i in range(4)]
        g = sb("g", [P, P])
        y = two("y", [P, TT, DIM])

        names = ["var_ready", "rstd_ready", "z_ready", "xn_ready", "front_ready",
                 "front_copied_act", "front_copied_dve", "square_ready", "square_summed", "mean_ready", "rk_ready",
                 "rq_ready", "kn_ready", "lc_ready", "cmax_ready", "cse_ready", "cp_ready",
                 "pool_front_step", "front_step", "scores_ready", "nbias_ready", "exp_done", "arg_ready",
                 "ecls_ready", "pt_ready", "pt_copied", "av_done", "o_copied", "attn_step", "pcls_ready",
                 "back_ready", "back_copied_act", "back_copied_dve", "var2_ready", "rstd2_ready",
                 "z2_ready", "hb_ready", "xr_copied", "relu_ready", "gate_summed", "back_step",
                 "group_step", "st_half"]
        s = {n: sem("i_" + n) for n in names}
        x_loaded, stored = ([sem(f"i_{n}{p}") for p in range(2)] for n in ("x_loaded", "stored"))
        front = Jobs(FRONT, [psum[5], psum[6]], s["front_ready"],
                     {"act": s["front_copied_act"], "dve": s["front_copied_dve"]})
        back = Jobs(BACK, [psum[7]], s["back_ready"],
                    {"act": s["back_copied_act"], "dve": s["back_copied_dve"]})
        heads = lambda ap: ap.rearrange("p (h d) -> p h d", d=DH)

        def images(eng, attention, frontwork, backwork):
            def slots(b, with_front=True, with_back=True):
                for slot in range(HEADS):
                    attention(b, slot)
                    if with_back:
                        backwork(b + -1, slot)
                    if with_front:
                        frontwork(b + 1, slot)

            for slot in range(HEADS):
                frontwork(At(0), slot)
            slots(At(0), with_back=False)
            slots(At(1))
            slots(At(2))
            if BATCHES > 4:
                with eng.Fori(0, BATCHES // 2 - 2) as i:
                    slots(At(3, i, 2))
                    slots(At(4, i, 2))
            slots(At(BATCHES - 1), with_front=False)
            for slot in range(HEADS):
                if slot < 2:
                    attention(At(BATCHES), slot, last=True)
                backwork(At(BATCHES - 1), slot)

        block = ctx.enter_context(nc.Block())

        @block.sync
        def _(sp):
            def load(b):
                wait(sp, s["xr_copied"], b, 1, -1)
                sp.dma_start(x[b.parity][:, :, :],
                             tokens[bass.ds(b.times(1), 1), :, :].rearrange("b (t p) l -> p (b t) l", p=P)
                             ).then_inc(x_loaded[b.parity], 16)

            def store(b):
                back.wait_copied(sp, b, "y")
                sp.dma_start(out[bass.ds(b.times(1), 1), 1:, :].rearrange("b (t p) l -> p (b t) l", p=P),
                             y[b.parity][:, :, :]).then_inc(stored[b.parity], 16)

            load(At(0))
            load(At(1))
            load(At(2))
            if BATCHES > 4:
                with sp.Fori(0, BATCHES // 2 - 2) as i:
                    for b in (At(3, i, 2), At(4, i, 2)):
                        load(b)
                        store(b + -3)
            load(At(BATCHES - 1))
            for b in range(BATCHES - 4, BATCHES):
                store(At(b))
            for p in range(2):
                sp.wait_ge(stored[p], 16 * (BATCHES // 2))

        @block.gpsimd
        def _(pool):
            step = Steps(pool, s["pool_front_step"], 12)

            def half_power(dst, src, ready):
                pool.tensor_tensor(dst, src, wt.half[:, 0:dst.shape[1]], ALU.pow).then_inc(ready, 1)

            def square(b, n, src):
                wait(pool, s["square_summed"], b, 8, n - 1)
                pool.tensor_tensor(sq[n % 2][:, :], src, src, ALU.mult).then_inc(s["square_ready"], 1)

            def scale_keys(b, half, t):
                cols = slice(half * 512, half * 512 + 512)
                kv = heads(ks[:, t, cols])
                pool.tensor_tensor(kv, kv, rk[:, t, half * 8:half * 8 + 8].unsqueeze(2).to_broadcast([P, 8, DH]),
                                   ALU.mult).then_inc(s["kn_ready"], 1)

            def front_work(b, slot):
                if slot == 0:
                    step.begin(b)
                    wait(pool, s["var_ready"], b, 1, 1)
                    half_power(rstd[:, :], mv[:, :, 1], s["rstd_ready"])
                if slot == 1:
                    wait(pool, s["z_ready"], b, TT, TT)
                    wn, bnn = (t[:, :].unsqueeze(1).to_broadcast([P, TT, DIM]) for t in (wt.ln_w, wt.ln_b))
                    step.did(pool.tensor_tensor(zn[:, :, :], zn[:, :, :], wn, ALU.mult))
                    step.settle()
                    pool.tensor_tensor(xn[b.parity][:, :, :], zn[:, :, :], bnn, ALU.add).then_inc(s["xn_ready"], 1)
                for n, name in enumerate(("k00", "k01", "k10", "k11")):
                    if slot == 4 + n:
                        front.wait_copied(pool, b, name)
                        square(b, n, ks[:, n % 2, n // 2 * 512:n // 2 * 512 + 512])
                if slot == 8:
                    wait(pool, s["mean_ready"], b, 2, 1)
                    half_power(rk[:, :, :].rearrange("p t h -> p (t h)"),
                               ss[:, 0, :, :].rearrange("p t h -> p (t h)"), s["rk_ready"])
                for n, name in enumerate(("q00", "q01", "q10", "q11")):
                    if slot == 9 + n:
                        front.wait_copied(pool, b, name)
                        square(b, 4 + n, qs[:, n % 2, n // 2 * 512:n // 2 * 512 + 512])
                if slot in (9, 10):
                    if slot == 9:
                        wait(pool, s["rk_ready"], b, 1, 1)
                    for t in range(TT):
                        scale_keys(b, slot - 9, t)
                if slot == 13:
                    wait(pool, s["mean_ready"], b, 2, 2)
                    half_power(rq[b.parity][:, :, :].rearrange("p t h -> p (t h)"),
                               ss[:, 1, :, :].rearrange("p t h -> p (t h)"), s["rq_ready"])

            def back_work(b, slot):
                if slot == 5:
                    wait(pool, s["var2_ready"], b, 1, 1)
                    half_power(rstd2[:, :], mv2[:, :, 1], s["rstd2_ready"])
                if slot == 6:
                    pool.tensor_tensor(hb[:, :, :], h1[:, :, :], wt.b_out[:, :].unsqueeze(1).to_broadcast([P, TT, DIM]),
                                       ALU.add).then_inc(s["hb_ready"], 1)

            step.per = 1
            images(pool, lambda b, slot, last=False: None, front_work, back_work)

        @block.tensor
        def _(pe):
            mm, tr = nc.tensor.matmul, nc.tensor.transpose

            def scores(b, h):
                par, pair, rows = b.parity, h // 2, slice((h % 2) * DH, (h % 2 + 1) * DH)
                if h == 0:
                    front.wait_copied(pe, b, "qt3")
                    front.wait_copied(pe, b, "kt3")
                wait(pe, s["exp_done"], b, 2 * HEADS, 2 * (h - 1))
                for t in range(TT):
                    last = mm(psum[h % 2][:, t * SEQ:(t + 1) * SEQ], qt[par][rows, pair, t * P:(t + 1) * P],
                              kt[par][rows, pair, :], start=True, stop=True)
                last.then_inc(s["scores_ready"], 1)

            def transpose_probs(b, h):
                wait(pe, s["exp_done"], b, 2 * HEADS, 2 * (h + 1))
                wait(pe, s["pt_copied"], b, HEADS, h - 1)
                for k in range(TT):
                    for t in range(TT):
                        last = tr(psum[2 + h % 2][:, (k * TT + t) * P:(k * TT + t + 1) * P],
                                  e[h % 2][:, t, k * P:(k + 1) * P], ident[:, :])
                last.then_inc(s["pt_ready"], 1)

            def values(b, h):
                wait(pe, s["pt_copied"], b, HEADS, h + 1)
                if h % 4 == 0:
                    wait(pe, s["o_copied"], b, GROUPS, h // 4)
                for t in range(TT):
                    for k in range(TT):
                        lo = (t * 4 + h % 4) * DH
                        last = mm(psum[4][:, lo:lo + DH], pt[h % 2][:, k, t * P:(t + 1) * P],
                                  v[b.parity][:, k, h * DH:(h + 1) * DH], start=(k == 0), stop=(k == TT - 1))
                last.then_inc(s["av_done"], 1)

            def attention(b, slot, last=False):
                if not last:
                    scores(b, slot)
                if slot >= 1:
                    transpose_probs(b, slot - 1) if not last else None
                elif not (b.reg is None and b.add == 0):
                    transpose_probs(b + -1, HEADS - 1)
                if slot >= 2:
                    values(b, slot - 2)
                elif not (b.reg is None and b.add == 0):
                    values(b + -1, HEADS - 2 + slot)

            def front_job(b, name):
                par, bank = b.parity, front.bank(name)
                front.wait_bank(pe, b, name)
                if name == "xt":
                    wait(pe, s["xn_ready"], b, 1, 1)
                    for c in range(LC):
                        for t in range(TT):
                            last = tr(bank[:, (c * TT + t) * P:(c * TT + t + 1) * P],
                                      xn[par][:, t, c * P:(c + 1) * P], ident[:, :])
                elif name[0] in "kqv" and name[1] in "01":
                    half, t = int(name[1]), int(name[2])
                    col = {"q": QC, "k": KC, "v": VC}[name[0]] + half * 512
                    if name == "k00":
                        front.wait_copied(pe, b, "xt")
                    for c in range(LC):
                        last = mm(bank[:, :], xnt[:, c, t * P:(t + 1) * P], wt.w[:, c, col:col + 512],
                                  start=(c == 0), stop=(c == LC - 1))
                elif name == "u":
                    for t in range(TT):
                        for c in range(LC):
                            last = mm(bank[:, t * 2 * HEADS:(t + 1) * 2 * HEADS], xnt[:, c, t * P:(t + 1) * P],
                                      wt.w[:, c, UC:UC + 2 * HEADS], start=(c == 0), stop=(c == LC - 1))
                elif name[:2] in ("kt", "qt"):
                    j = int(name[2])
                    if name[0] == "k":
                        wait(pe, s["kn_ready"], b, 4, 2 * (j // 2) + 2)
                        src = ks
                    else:
                        front.wait_copied(pe, b, f"q{j // 2}1")
                        src = qs
                    for pr in range(2):
                        for t in range(TT):
                            lo = (2 * j + pr) * P
                            last = tr(bank[:, (pr * TT + t) * P:(pr * TT + t + 1) * P], src[:, t, lo:lo + P],
                                      ident[:, :])
                elif name == "lc":
                    wait(pe, s["lc_ready"], b, 1, 1)
                    for t in range(TT):
                        last = tr(bank[0:HEADS, t * P:(t + 1) * P], lc[:, t, :], ident[:, :])
                elif name == "pc":
                    wait(pe, s["cp_ready"], b, 1, 1)
                    for t in range(TT):
                        last = mm(bank[:, t * HEADS:(t + 1) * HEADS], cp[:, t * P:(t + 1) * P],
                                  ident[0:HEADS, 0:HEADS], start=True, stop=True)
                elif name == "xb":
                    front.wait_copied(pe, b, "pc")
                    for c in range(LC):
                        for t in range(TT):
                            last = mm(bank[:, c * HEADS:(c + 1) * HEADS], xn[par][:, t, c * P:(c + 1) * P],
                                      cpt[:, t, :], start=(t == 0), stop=(t == TT - 1))
                last.then_inc(s["front_ready"], 1)

            def back_job(b, name):
                bank = back.bank(name)
                back.wait_bank(pe, b, name)
                if name[:2] == "ot":
                    j = int(name[2])
                    wait(pe, s["o_copied"], b, GROUPS, j + 1)
                    for pr in range(2):
                        for t in range(TT):
                            lo = (2 * j + pr) * P
                            last = tr(bank[:, (pr * TT + t) * P:(pr * TT + t + 1) * P], o[:, t, lo:lo + P],
                                      ident[:, :])
                elif name == "pt":
                    wait(pe, s["pcls_ready"], b, 1, 1)
                    for t in range(TT):
                        last = tr(bank[0:HEADS, t * P:(t + 1) * P], pcls[:, t, :], ident[:, :])
                elif name == "wo":
                    back.wait_copied(pe, b, "ot3")
                    for t in range(TT):
                        dst = bank[:, t * DIM:(t + 1) * DIM]
                        for c in range(PAIRS):
                            mm(dst, ot[:, c, t * P:(t + 1) * P], wt.wo[:, c, :], start=(c == 0), stop=False)
                        last = mm(dst, pclst[:, t * P:(t + 1) * P], wt.z[:, :], start=False, stop=True)
                elif name == "z2t":
                    wait(pe, s["z2_ready"], b, TT, TT)
                    for c in range(LC):
                        for t in range(TT):
                            last = tr(bank[:, (c * TT + t) * P:(c * TT + t + 1) * P], z2[:, t, c * P:(c + 1) * P],
                                      ident[:, :])
                elif name == "s":
                    for c in range(LC):
                        last = mm(bank[:, 0:SEQ], wt.w_in[:, c, :], yt[:, c, :], start=(c == 0), stop=(c == LC - 1))
                elif name == "y":
                    wait(pe, s["gate_summed"], b, MI, MI)
                    for t in range(TT):
                        last = mm(bank[:, t * DIM:(t + 1) * DIM], g[:, :], wt.w_out[:, t, :],
                                  start=True, stop=True)
                last.then_inc(s["back_ready"], 1)

            images(pe, attention,
                   lambda b, slot: [front_job(b, n) for n in front.in_slot(slot)],
                   lambda b, slot: [back_job(b, n) for n in back.in_slot(slot)])

        @block.scalar
        def _(act):
            run = nc.scalar.activation

            def attention(b, slot, last=False):
                h = slot
                if h % 4 == 0 and not (b.reg is None and b.add == 0 and h == 0):
                    pb, q = (b, h // 4 - 1) if h else (b + -1, GROUPS - 1)
                    wait(act, s["arg_ready"], pb, GROUPS, q + 1)
                    cols = slice(4 * q, 4 * q + 4)
                    run(ecls[:, :, cols], earg[:, :, cols], ACT.Exp).then_inc(s["ecls_ready"], 1)
                if last:
                    return
                wait(act, s["nbias_ready"], b, HEADS, h + 1)
                wait(act, s["pt_ready"], b, HEADS, h - 1)
                for t in range(TT):
                    run(e[h % 2][:, t, :], psum[h % 2][:, t * SEQ:(t + 1) * SEQ], ACT.Exp,
                        scale=rq[b.parity][:, t, h:h + 1], bias=nb[:, t, h:h + 1],
                        accum_out=esum[:, t, h:h + 1]).then_inc(s["exp_done"], 1)

            def front_job(b, name):
                par, bank = b.parity, front.bank(name)
                front.wait_ready(act, b, name)
                if name[0] in "kqv" and name[1] in "01":
                    half, t = int(name[1]), int(name[2])
                    dst = {"q": qs, "k": ks, "v": v[par]}[name[0]]
                    ins = run(dst[:, t, half * 512:half * 512 + 512], bank[:, :], ACT.Copy)
                elif name[:2] == "qt":
                    j = int(name[2])
                    ins = run(qt[par][:, 2 * j:2 * j + 2, :].rearrange("p c t -> p (c t)"), bank[:, :], ACT.Copy)
                else:
                    wait(act, s["cmax_ready"], b, 1, 1)
                    ins = run(ce[:, :], bank[0:HEADS, 0:SEQ], ACT.Exp, bias=ncm[:, 0:1], accum_out=cs[:, 0:1])
                ins.then_inc(s["front_copied_act"], 1)
                if name == "lc":
                    run(cse[:, :], wt.scc[:, :], ACT.Exp, bias=ncm[:, 0:1]).then_inc(s["cse_ready"], 1)

            def back_job(b, name):
                bank = back.bank(name)
                back.wait_ready(act, b, name)
                if name == "s":
                    for t in range(TT):
                        rows = slice(t * M, (t + 1) * M)
                        ins = run(st[rows, :], bank[rows, t * P:(t + 1) * P], ACT.Identity, bias=wt.b_in[rows, 0:1])
                        if t == 0:
                            ins.then_inc(s["st_half"], 1)
                else:
                    j = int(name[2])
                    ins = run(ot[:, 2 * j:2 * j + 2, :].rearrange("p c t -> p (c t)"), bank[:, :], ACT.Copy)
                ins.then_inc(s["back_copied_act"], 1)

            def back_work(b, slot):
                for n in back.in_slot(slot, "act"):
                    back_job(b, n)
                if 10 <= slot < 14:
                    if slot == 10:
                        back.wait_copied(act, b, "s")
                        wait(act, s["st_half"], b, 1, 1)
                    for i in range(4 * (slot - 10), 4 * (slot - 10) + 4):
                        wait(act, s["gate_summed"], b, MI, i - 3)
                        run(relu[i % 4][:, :], st[:, :], ACT.Relu, scale=wt.w1[:, i:i + 1],
                            bias=wt.b1[:, i:i + 1]).then_inc(s["relu_ready"], 1)

            images(act, attention,
                   lambda b, slot: [front_job(b, n) for n in front.in_slot(slot, "act")], back_work)

        @block.vector
        def _(dve):
            tt, ts = nc.vector.tensor_tensor, nc.vector.tensor_scalar
            fs = Steps(dve, s["front_step"], 13)
            bs = Steps(dve, s["back_step"], 4)
            at = Steps(dve, s["attn_step"], 40)

            def normalise_stats(src, stats, mean_var, step):
                for t in range(TT):
                    step.did(nc.vector.bn_stats(stats[:, t, :], src[:, t, :]))
                step.settle()
                step.did(nc.vector.memset(carrier[:, :], 0.0))
                for t in range(TT):
                    step.did(nc.vector.bn_aggr(mean_var[:, t, :], stats[:, t, :]))
                step.settle()
                return mean_var[:, :, 1]

            def max_and_bias(b, h):
                wait(dve, s["scores_ready"], b, HEADS, h + 1)
                at.did(nc.vector.tensor_reduce(mx[:, :], psum[h % 2][:, :].rearrange("p (t k) -> p t k", t=TT),
                                               AX.X, ALU.max))
                at.settle()
                at.did(tt(mxc[:, :], mx[:, :], u[b.parity][:, :, HEADS + h], ALU.max))
                at.settle()
                tt(nb[:, :, h], mxc[:, :], nrq[:, :, h], ALU.mult).then_inc(s["nbias_ready"], 1)
                if h % 4 == 3:
                    cols = slice(h - 3, h + 1)
                    wait(dve, s["nbias_ready"], b, HEADS, h + 1)
                    tt(earg[:, :, cols], ru[:, :, cols], nb[:, :, cols], ALU.add).then_inc(s["arg_ready"], 1)

            def copy_probs(b, h):
                wait(dve, s["pt_ready"], b, HEADS, h + 1)
                nc.vector.tensor_copy(pt[h % 2][:, :, :].rearrange("p k q -> p (k q)"),
                                      psum[2 + h % 2][:, :]).then_inc(s["pt_copied"], 1)

            def output_group(b, q):
                cols = slice(4 * q, 4 * q + 4)
                wait(dve, s["ecls_ready"], b, GROUPS, q + 1)
                tt(den[:, :, :], esum[:, :, cols], ecls[:, :, cols], ALU.add).then_inc(s["group_step"], 1)
                wait(dve, s["group_step"], b, 2 * GROUPS, 2 * q + 1)
                nc.vector.reciprocal(rinv[:, :, cols], den[:, :, :]).then_inc(s["group_step"], 1)
                wait(dve, s["group_step"], b, 2 * GROUPS, 2 * q + 2)
                wait(dve, s["av_done"], b, HEADS, 4 * q + 4)
                tt(o[:, :, q * 4 * DH:(q + 1) * 4 * DH].rearrange("p t (h d) -> p t h d", d=DH),
                   psum[4][:, :].rearrange("p (t h d) -> p t h d", t=TT, d=DH),
                   rinv[:, :, cols].unsqueeze(3).to_broadcast([P, TT, 4, DH]), ALU.mult).then_inc(s["o_copied"], 1)

            def attention(b, slot, last=False):
                started = b.reg is not None or b.add > 0
                if slot == 0 and not last:
                    at.begin(b)
                    wait(dve, s["rq_ready"], b, 1, 1)
                    wait(dve, s["arg_ready"], b, GROUPS, 0)
                    at.did(ts(nrq[:, :, :], rq[b.parity][:, :, :], -1.0, None, ALU.mult))
                    at.did(tt(ru[:, :, :], rq[b.parity][:, :, :], u[b.parity][:, :, HEADS:], ALU.mult))
                    at.settle()
                if not last:
                    max_and_bias(b, slot)
                if slot == 0 and started:
                    copy_probs(b + -1, HEADS - 1)
                elif slot > 0 and not last:
                    copy_probs(b, slot - 1)
                if slot == 1 and started:
                    output_group(b + -1, GROUPS - 1)
                    tt(pcls[:, :, :], ecls[:, :, :], rinv[:, :, :], ALU.mult).then_inc(s["pcls_ready"], 1)
                elif slot % 4 == 1 and slot > 1:
                    output_group(b, slot // 4 - 1)
                if slot == 7 and not last:
                    back.wait_copied(dve, b + -1, "wo")
                    nc.vector.tensor_copy(xr[:, :, :], x[b.parity][:, :, :]).then_inc(s["xr_copied"], 1)

            def front_job(b, name):
                par, bank = b.parity, front.bank(name)
                front.wait_ready(dve, b, name)
                if name == "xt":
                    ins = nc.vector.tensor_copy(xnt[:, :, :].rearrange("p c t -> p (c t)"), bank[:, :])
                elif name == "u":
                    ins = nc.vector.tensor_copy(u[par][:, :, :].rearrange("p t h -> p (t h)"), bank[:, 0:TT * 2 * HEADS])
                elif name[:2] == "kt":
                    j = int(name[2])
                    for pr in range(2):
                        ins = ts(kt[par][:, 2 * j + pr, :], bank[:, pr * SEQ:(pr + 1) * SEQ],
                                 wt.gam[:, 2 * j + pr:2 * j + pr + 1], None, ALU.mult)
                        if pr == 0:
                            fs.did(ins)
                elif name == "pc":
                    ins = nc.vector.tensor_copy(cpt[:, :, :].rearrange("p t h -> p (t h)"), bank[:, 0:TT * HEADS])
                else:
                    ins = nc.vector.tensor_copy(xb[:, bass.ds(b.times(1), 1), :].rearrange("p b n -> p (b n)"),
                                                bank[:, 0:LC * HEADS])
                ins.then_inc(s["front_copied_dve"], 1)

            def front_work(b, slot):
                par = b.parity
                if slot == 0:
                    fs.begin(b)
                    wait(dve, x_loaded[par], b.half, 16, 16)
                    var = normalise_stats(x[par], bn, mv, fs)
                    ts(var, var, 1.0 + LN_EPS, LN_EPS * LN_EPS, ALU.mult, ALU.add).then_inc(s["var_ready"], 1)
                if slot == 1:
                    wait(dve, s["rstd_ready"], b, 1, 1)
                    wait(dve, s["xn_ready"], b, 1, 0)
                    for t in range(TT):
                        ts(zn[:, t, :], x[par][:, t, :], mv[:, t, 0:1], rstd[:, t:t + 1],
                           ALU.subtract, ALU.mult).then_inc(s["z_ready"], 1)
                if 5 <= slot < 9 or 10 <= slot < 14:
                    n = slot - 5 if slot < 9 else slot - 6
                    which, half, t = n // 4, n % 4 // 2, n % 2
                    wait(dve, s["square_ready"], b, 8, n + 1)
                    nc.vector.tensor_reduce(ss[:, which, t, half * 8:half * 8 + 8], heads(sq[n % 2][:, :]),
                                            AX.X, ALU.add).then_inc(s["square_summed"], 1)
                    if n % 4 == 3:
                        wait(dve, s["square_summed"], b, 8, n + 1)
                        f = ss[:, which, :, :]
                        ts(f, f, 1.0 / DH, RMS_EPS, ALU.mult, ALU.add).then_inc(s["mean_ready"], 1)
                if slot == 10:
                    wait(dve, s["rk_ready"], b, 1, 1)
                    front.wait_copied(dve, b, "u")
                    tt(lc[:, :, :], rk[:, :, :], u[par][:, :, 0:HEADS], ALU.mult).then_inc(s["lc_ready"], 1)
                if slot == 11:
                    front.wait_ready(dve, b, "lc")
                    fs.did(nc.vector.tensor_reduce(cm[:, :], front.bank("lc")[0:HEADS, 0:SEQ], AX.X, ALU.max))
                    fs.settle()
                    ts(ncm[:, :], cm[:, :], wt.scc[:, 0:1], -1.0, ALU.max, ALU.mult).then_inc(s["cmax_ready"], 1)
                if slot == 12:
                    wait(dve, s["cse_ready"], b, 1, 1)
                    fs.did(tt(csum[:, :], cs[:, :], cse[:, :], ALU.add))
                    fs.settle()
                    fs.did(nc.vector.reciprocal(cinv[:, :], csum[:, :]))
                    fs.settle()
                    fs.did(tt(pcc[:, bass.ds(b.times(1), 1)], cse[:, :], cinv[:, :], ALU.mult))
                    ts(cp[:, :], ce[:, :], cinv[:, 0:1], None, ALU.mult).then_inc(s["cp_ready"], 1)
                for n in front.in_slot(slot, "dve"):
                    front_job(b, n)
                if slot == 15:
                    fs.end()

            def back_work(b, slot):
                if slot == 0:
                    bs.begin(b)
                if slot == 3:
                    back.wait_ready(dve, b, "pt")
                    nc.vector.tensor_copy(pclst[:, :], psum[7][0:HEADS, 0:SEQ]).then_inc(s["back_copied_dve"], 1)
                if slot == 4:
                    back.wait_ready(dve, b, "wo")
                    wait(dve, s["xr_copied"], b, 1, 1)
                    tt(h1[:, :, :].rearrange("p t l -> p (t l)"), psum[7][:, :],
                       xr[:, :, :].rearrange("p t l -> p (t l)"), ALU.add).then_inc(s["back_copied_dve"], 1)
                    back.wait_copied(dve, b, "wo")
                    var = normalise_stats(h1, bn2, mv2, bs)
                    ts(var, var, LN_EPS, None, ALU.add).then_inc(s["var2_ready"], 1)
                if slot == 7:
                    wait(dve, s["rstd2_ready"], b, 1, 1)
                    for t in range(TT):
                        ts(z2[:, t, :], h1[:, t, :], mv2[:, t, 0:1], rstd2[:, t:t + 1],
                           ALU.subtract, ALU.mult).then_inc(s["z2_ready"], 1)
                if slot == 8:
                    back.wait_ready(dve, b, "z2t")
                    nc.vector.tensor_copy(yt[:, :, :].rearrange("p c t -> p (c t)"),
                                          psum[7][:, :]).then_inc(s["back_copied_dve"], 1)
                if 10 <= slot < 14:
                    for i in range(4 * (slot - 10), 4 * (slot - 10) + 4):
                        wait(dve, s["relu_ready"], b, MI, i + 1)
                        wait(dve, s["gate_summed"], b, MI, i)
                        if i == 0:
                            ins = ts(g[:, :], relu[0][:, :], wt.w2[:, 0:1], wt.b2[:, 0:1], ALU.mult, ALU.add)
                        else:
                            ins = nc.vector.scalar_tensor_tensor(g[:, :], relu[i % 4][:, :], wt.w2[:, i:i + 1], g[:, :],
                                                                 ALU.mult, ALU.add)
                        ins.then_inc(s["gate_summed"], 1)
                if slot == 15:
                    back.wait_ready(dve, b, "y")
                    wait(dve, s["hb_ready"], b, 1, 1)
                    wait(dve, stored[b.parity], b.half, 16, 0)
                    yv = y[b.parity]
                    tt(yv[:, :, :].rearrange("p t l -> p (t l)"), psum[7][:, :],
                       hb[:, :, :].rearrange("p t l -> p (t l)"), ALU.add).then_inc(s["back_copied_dve"], 1)
                    bs.end()

            fs.per, bs.per, at.per = 13, 5, 2 + 2 * HEADS
            images(dve, attention, front_work, back_work)



def class_rows_program(nc, psum, ident, wt, xb, pcc, out):
    B = BATCHES
    ctx = ExitStack()
    with ctx:
        def sb(name, shape):
            return ctx.enter_context(nc.sbuf_tensor("r_" + name, shape, F32))

        def sem(name):
            return ctx.enter_context(nc.semaphore("r_" + name))

        pc = sb("pc", [B, HEADS])
        oc = sb("oc", [B, INNER])
        ot = sb("ot", [P, PAIRS, B])
        h1 = sb("h1", [B, DIM])
        bn = sb("bn", [B, 6])
        mv = sb("mv", [B, 2])
        rstd = sb("rstd", [B, 1])
        z = sb("z", [B, DIM])
        zt = sb("zt", [P, LC, B])
        st = sb("st", [M, B])
        term = sb("term", [M, MI, B])
        g = sb("g", [M, B])
        y = sb("y", [B, DIM])
        pe_step, dve_step, act_step = sem("pe_step"), sem("dve_step"), sem("act_step")
        oc_ready, ot_ready, var_ready, rstd_ready = sem("oc_ready"), sem("ot_ready"), sem("var_ready"), sem("rstd_ready")
        z_ready, zt_ready, g_ready, y_ready, stored = (sem(n) for n in ("z_ready", "zt_ready", "g_ready", "y_ready", "stored"))
        block = ctx.enter_context(nc.Block())

        @block.sync
        def _(sp):
            sp.wait_ge(y_ready, 1)
            sp.dma_start(out[:, 0, :], y[:, :]).then_inc(stored, 16)
            sp.wait_ge(stored, 16)

        @block.gpsimd
        def _(pool):
            pool.wait_ge(var_ready, 1)
            pool.tensor_tensor(rstd[:, :], mv[:, 1:2], wt.half[0:B, 0:1], ALU.pow).then_inc(rstd_ready, 1)

        @block.tensor
        def _(pe):
            mm, tr = nc.tensor.matmul, nc.tensor.transpose
            tr(psum[0][0:B, 0:HEADS], pcc[:, :], ident[0:HEADS, 0:HEADS]).then_inc(pe_step, 1)
            for h in range(HEADS):
                bank, lo = psum[1 + h // 8], h % 8 * DH
                for c in range(LC):
                    last = mm(bank[0:B, lo:lo + DH], xb[:, :, c * HEADS + h],
                              wt.w[:, c, VC + h * DH:VC + (h + 1) * DH], start=(c == 0), stop=(c == LC - 1))
            last.then_inc(pe_step, 1)
            pe.wait_ge(oc_ready, 1)
            for c in range(PAIRS):
                last = tr(psum[3][:, c * B:(c + 1) * B], oc[:, c * P:(c + 1) * P], ident[0:B, 0:B])
            last.then_inc(pe_step, 1)
            pe.wait_ge(ot_ready, 1)
            for c in range(PAIRS):
                last = mm(psum[4][0:B, 0:DIM], ot[:, c, :], wt.wo[:, c, :], start=(c == 0), stop=(c == PAIRS - 1))
            last.then_inc(pe_step, 1)
            pe.wait_ge(z_ready, 1)
            for c in range(LC):
                last = tr(psum[5][:, c * B:(c + 1) * B], z[:, c * P:(c + 1) * P], ident[0:B, 0:B])
            last.then_inc(pe_step, 1)
            pe.wait_ge(zt_ready, 1)
            for c in range(LC):
                last = mm(psum[6][0:M, 0:B], wt.w_in[:, c, 0:M], zt[:, c, :], start=(c == 0), stop=(c == LC - 1))
            last.then_inc(pe_step, 1)
            pe.wait_ge(g_ready, 1)
            mm(psum[7][0:B, 0:DIM], g[:, :], wt.w_out[0:M, 0, :], start=True, stop=True).then_inc(pe_step, 1)

        @block.scalar
        def _(act):
            act.wait_ge(pe_step, 6)
            nc.scalar.activation(st[:, :], psum[6][0:M, 0:B], ACT.Identity, bias=wt.b_in[0:M, 0:1]).then_inc(act_step, 1)
            act.wait_ge(act_step, 1)
            for i in range(MI):
                nc.scalar.activation(term[:, i, :], st[:, :], ACT.Relu, scale=wt.w1[0:M, i:i + 1],
                                     bias=wt.b1[0:M, i:i + 1]).then_inc(act_step, 1)

        @block.vector
        def _(dve):
            count = [0]

            def link(ins):
                count[0] += 1
                ins.then_inc(dve_step, 1)
                dve.wait_ge(dve_step, count[0])

            tt, ts = nc.vector.tensor_tensor, nc.vector.tensor_scalar
            dve.wait_ge(pe_step, 1)
            link(nc.vector.tensor_copy(pc[:, :], psum[0][0:B, 0:HEADS]))
            link(tt(oc[:, :].rearrange("b (h d) -> b h d", d=DH), wt.v_cls[0:B, :].rearrange("b (h d) -> b h d", d=DH),
                    pc[:, :].unsqueeze(2).to_broadcast([B, HEADS, DH]), ALU.mult))
            dve.wait_ge(pe_step, 2)
            for j in range(2):
                ins = tt(oc[:, j * 512:(j + 1) * 512], oc[:, j * 512:(j + 1) * 512], psum[1 + j][0:B, :], ALU.add)
                if j == 0:
                    link(ins)
                else:
                    ins.then_inc(oc_ready, 1)
            dve.wait_ge(pe_step, 3)
            nc.vector.tensor_copy(ot[:, :, :].rearrange("p c b -> p (c b)"), psum[3][:, 0:PAIRS * B]).then_inc(ot_ready, 1)
            dve.wait_ge(pe_step, 4)
            link(tt(h1[:, :], psum[4][0:B, 0:DIM], wt.cls[0:B, :], ALU.add))
            link(nc.vector.bn_stats(bn[:, :], h1[:, :]))
            link(nc.vector.bn_aggr(mv[:, :], bn[:, :]))
            ts(mv[:, 1:2], mv[:, 1:2], LN_EPS, None, ALU.add).then_inc(var_ready, 1)
            dve.wait_ge(rstd_ready, 1)
            ts(z[:, :], h1[:, :], mv[:, 0:1], rstd[:, 0:1], ALU.subtract, ALU.mult).then_inc(z_ready, 1)
            link(tt(h1[:, :], h1[:, :], wt.b_out[0:B, :], ALU.add))
            dve.wait_ge(pe_step, 5)
            nc.vector.tensor_copy(zt[:, :, :].rearrange("p c b -> p (c b)"), psum[5][:, 0:LC * B]).then_inc(zt_ready, 1)
            dve.wait_ge(act_step, 2)
            link(ts(g[:, :], term[:, 0, :], wt.w2[0:M, 0:1], wt.b2[0:M, 0:1], ALU.mult, ALU.add))
            for i in range(1, MI):
                dve.wait_ge(act_step, i + 2)
                ins = nc.vector.scalar_tensor_tensor(g[:, :], term[:, i, :], wt.w2[0:M, i:i + 1], g[:, :], ALU.mult, ALU.add)
                if i < MI - 1:
                    link(ins)
                else:
                    ins.then_inc(g_ready, 1)
            dve.wait_ge(pe_step, 7)
            tt(y[:, :], psum[7][0:B, 0:DIM], h1[:, :], ALU.add).then_inc(y_ready, 1)



def tower(nc, x, cls_tok, log_dt, inv_a, a_imag, b_ri, ln_w, ln_b, wq, wkv, q_gamma, k_gamma, wo,
          w_in, b_in, w1, b1, w2, b2, w_out, b_out, out):
    tokens = nc.dram_tensor("tokens", (NC, SEQ, DIM), F32, kind="Internal").ap()
    ctx = ExitStack()
    with ctx:
        psum = [ctx.enter_context(nc.psum_tensor(f"bank{i}", [P, 512], F32)) for i in range(8)]
        ident = ctx.enter_context(nc.sbuf_tensor("ident", [P, P], F32))
        ident_ready = ctx.enter_context(nc.semaphore("ident_ready"))
        with nc.Block() as block:
            @block.gpsimd
            def _(pool):
                pool.memset(ident[:, :], 0.0).then_inc(ident_ready, 1)
                pool.wait_ge(ident_ready, 1)
                pool.affine_select(out=ident[:, :], in_=ident[:, :], compare_op=ALU.not_equal, fill=1.0,
                                   base=0, pattern=[[-1, P]], channel_multiplier=1).then_inc(ident_ready, 1)
                pool.wait_ge(ident_ready, 2)
        wt = Weights(nc, ctx)
        class_program(nc, psum, ident, wt, cls_tok, ln_w, ln_b, wq, wkv, q_gamma, k_gamma, wo,
                      w_in, b_in, w1, b1, w2, b2, w_out, b_out)
        token_program(nc, psum, ident, x, log_dt, inv_a, a_imag, b_ri, tokens)
        pcc = ctx.enter_context(nc.sbuf_tensor("pcc", [HEADS, BATCHES], F32))
        xb = ctx.enter_context(nc.sbuf_tensor("xb", [P, BATCHES, LC * HEADS], F32))
        image_program(nc, psum, ident, wt, tokens, xb, pcc, out)
        class_rows_program(nc, psum, ident, wt, xb, pcc, out)



INPUTS = ['x', 'cls_tok', 'L0_tok_log_dt', 'L0_tok_inv_A_real', 'L0_tok_A_imag', 'L0_tok_B_ri',
          'L0_attn_ln_w', 'L0_attn_ln_b', 'L0_attn_Wq', 'L0_attn_Wkv', 'L0_attn_q_gamma', 'L0_attn_k_gamma',
          'L0_attn_Wo', 'L0_ffn_Win', 'L0_ffn_bin_', 'L0_ffn_W1', 'L0_ffn_b1', 'L0_ffn_W2', 'L0_ffn_b2',
          'L0_ffn_Wout', 'L0_ffn_bout']


def kernel(**inputs):
    import numpy as np
    import concourse.bacc as bacc
    from concourse import mybir as mb
    from concourse.bass_utils import run_bass_kernel_spmd

    nc = bacc.Bacc("TRN2", target_bir_lowering=False, num_devices=1)
    arrays, args = {}, []
    for name in INPUTS:
        a = np.ascontiguousarray(inputs[name])
        arrays[name] = a
        args.append(nc.dram_tensor(name, a.shape, mb.dt.from_np(a.dtype), kind="ExternalInput").ap())
    out = nc.dram_tensor("out", (BATCHES, SEQ + 1, DIM), mb.dt.float32, kind="ExternalOutput").ap()
    tower(nc, *args, out)
    r = run_bass_kernel_spmd(nc, [arrays], core_ids=[0])
    return r.results[0]["out"]
```

```python
from contextlib import ExitStack

import concourse.bass as bass
from concourse import mybir

F32 = mybir.dt.float32
F16 = mybir.dt.float16
I32 = mybir.dt.int32
RMAX = bass.bass_isa.ReduceOp.max
ALU = mybir.AluOpType
ACT = mybir.ActivationFunctionType
AX = mybir.AxisListType

BATCHES = 32
P = 128
SEQ = 256
DIM = 256
NST = 64
HEADS, DH = 16, 64
INNER = HEADS * DH
TT = SEQ // P
LC = DIM // P
PAIRS = INNER // P
GROUPS = 4
M, MI = 64, 16
LN_EPS = 1e-5
RMS_EPS = 1e-8
HALVES = 4
STEP = DIM // HALVES
NC = 32
CHUNK = 16
QC, KC, VC, UC = 0, INNER, 2 * INNER, 3 * INNER
WCOLS = 3 * INNER + 2 * HEADS


class At:

    def __init__(self, add, reg=None, mul=0):
        self.add, self.reg, self.mul = add, reg, mul

    def __add__(self, n):
        return At(self.add + n, self.reg, self.mul)

    @property
    def parity(self):
        return self.add % 2

    @property
    def half(self):
        return At(self.add // 2, self.reg, self.mul // 2)

    def times(self, k):
        return self.add * k if self.reg is None else self.reg * (self.mul * k) + self.add * k


def wait(eng, sem, b, per, n):
    const = b.add * per + n
    if b.reg is None:
        if const > 0:
            eng.wait_ge(sem, const)
    else:
        assert const > 0
        eng.wait_ge(sem, b.reg * (b.mul * per) + const)


class Steps:

    def __init__(self, eng, sem, per):
        self.eng, self.sem, self.per, self.b, self.n = eng, sem, per, At(0), 0

    def begin(self, b):
        self.b, self.n = b, 0

    def did(self, ins):
        self.n += 1
        ins.then_inc(self.sem, 1)

    def settle(self):
        wait(self.eng, self.sem, self.b, self.per, self.n)

    def end(self):
        assert self.n == self.per, (self.n, self.per)



def token_program(nc, psum, ident, x, log_dt, inv_a, a_imag, b_ri, tokens, wt, load_weights):
    chunks = P // CHUNK
    ctx = ExitStack()
    with ctx:
        def sb(name, shape):
            return ctx.enter_context(nc.sbuf_tensor(name, shape, F32))

        def sem(name):
            return ctx.enter_context(nc.semaphore(name))

        dt_in = sb("dt_in", [P, 2])
        dt = sb("dt", [P, 2])
        e_const = sb("e_const", [P, 2])
        are = sb("are", [P, 2, NST])
        aim = sb("aim", [P, 2, NST])
        bri = sb("bri", [P, 2, NST, 2])
        half_re = sb("half_re", [P, 2, NST])
        half_im = sb("half_im", [P, 2, NST])
        t0 = sb("t0", [P, P])
        t1 = sb("t1", [P, P])
        t2 = sb("t2", [P, P])
        xc = [sb(f"xc{i}", [P, 8, 2 * 2 * NST]) for i in range(2)]
        ct = sb("ct", [P, 2, P, NC])
        pw = sb("pw", [P, 6, 2, P])
        big = sb("big", [P, 3, 2, P])
        bp = sb("bp", [P, 4, P, HALVES])
        prod = [sb(f"prod{i}", [P, CHUNK * HALVES * NC]) for i in range(2)]
        cp = [sb(f"cp{i}", [P, 2, CHUNK, HALVES * NC]) for i in range(2)]
        qp = [sb(f"qp{i}", [P, 2, CHUNK, STEP]) for i in range(2)]
        qt = [sb(f"qt{i}", [P, CHUNK * STEP // 2]) for i in range(2)]
        qd = sb("qd", [P, 12, CHUNK])
        ko = [sb(f"ko{i}", [P, 8, STEP]) for i in range(4)]
        nat = ko[0][:, :, :].rearrange("p h b -> p (h b)").rearrange("p (i h) -> p i h", i=4)

        params_in = sem("params_in")
        c_in = [sem(f"c_in{i}") for i in range(4)]
        dt_ready = sem("dt_ready")
        exp_ready = sem("exp_ready")
        nat_ready = sem("nat_ready")
        nat_t = sem("nat_t")
        c_t = sem("c_t")
        c_copied = sem("c_copied")
        powers_ready = sem("powers_ready")
        dve_step = sem("tok_dve_step")
        pool_step = sem("tok_pool_step")
        cp_ready = sem("cp_ready")
        qp_ready = sem("qp_ready")
        mm_done = sem("mm_done")
        cp_re_ready = sem("cp_re_ready")
        ko_ready = sem("ko_ready")
        stored = [sem(f"stored{i}") for i in range(4)]
        block = ctx.enter_context(nc.Block())
        jobs = 4

        @block.sync
        def _(sp):
            for g in range(2):
                sp.dma_start(dt_in[:, g:g + 1], log_dt[g * P:(g + 1) * P].unsqueeze(1)).then_inc(params_in, 16)
            sp.dma_start(are[:, :, :], inv_a.rearrange("(g p) n -> p g n", g=2)).then_inc(params_in, 16)
            sp.dma_start(aim[:, :, :], a_imag.rearrange("(g p) n -> p g n", g=2)).then_inc(params_in, 16)
            sp.dma_start(bri[:, :, :, :], b_ri.rearrange("(g p) n r -> p g n r", g=2)).then_inc(params_in, 16)
            for i in range(4):
                cs = slice(i * 8, i * 8 + 8)
                if i >= 2:
                    sp.wait_ge(c_t, 16 * (i - 1))
                for g in range(2):
                    sp.dma_start(xc[i % 2][:, :, g * P:(g + 1) * P],
                                 x[cs, g * P:(g + 1) * P].rearrange("c p n r -> p c (n r)")).then_inc(c_in[i], 16)
            load_weights(sp)
            with sp.Fori(0, chunks) as k:
                for j in range(jobs):
                    sp.wait_ge(ko_ready, k * jobs + (j + 1))
                    g, half = j // 2, j % 2
                    for a in range(HALVES):
                        dst = tokens[:, bass.ds(k * CHUNK + (g * P + half * 8), 8), a * STEP:(a + 1) * STEP]
                        sp.dma_start(dst, ko[j][a * NC:(a + 1) * NC, :, :]).then_inc(stored[j], 16)
            for j in range(4):
                sp.wait_ge(stored[j], 16 * HALVES * chunks)

        @block.scalar
        def _(act):
            act.wait_ge(params_in, 80)
            nc.scalar.activation(half_re[:, :, :], are[:, :, :], ACT.Exp).then_inc(exp_ready, 1)
            for j in range(16):
                r, c0 = j % 2, 4 * (j // 2)
                act.wait_ge(c_t, 4 * j + 4)
                nc.scalar.activation(ct[:, r, :, c0:c0 + 4],
                                     psum[1 + j % 2][:, :].rearrange("p (c h) -> p h c", c=4),
                                     ACT.Copy).then_inc(c_copied, 1)
            def features_out(k):
                for j in range(jobs):
                    wait(act, mm_done, k, jobs, j + 1)
                    wait(act, stored[j], k, 16 * HALVES, 0)
                    nc.scalar.activation(ko[j][:, :, :],
                                         psum[3 + j][:, :].rearrange("p (h b) -> p h b", h=8),
                                         ACT.Copy).then_inc(ko_ready, 1)

            features_out(At(0))
            with act.Fori(0, chunks - 1) as k:
                features_out(At(1, k, 1))

        @block.tensor
        def _(pe):
            pe.wait_ge(nat_ready, 1)
            for i in range(4):
                nc.tensor.transpose(psum[0][:, i * P:(i + 1) * P], nat[:, i, :], ident[:, :]).then_inc(nat_t, 1)
            for j in range(16):
                r, c0 = j % 2, 4 * (j // 2)
                if j % 4 == 0:
                    pe.wait_ge(c_in[j // 4], 32)
                if j >= 2:
                    pe.wait_ge(c_copied, j - 1)
                for c in range(4):
                    nc.tensor.transpose(psum[1 + j % 2][:, c * P:(c + 1) * P],
                                        xc[j // 4 % 2][:, (c0 + c) % 8, r::2], ident[:, :]).then_inc(c_t, 1)

            def product(k):
                par = k.parity
                wait(pe, cp_ready, k, 1, 1)
                wait(pe, qp_ready, k, 1, 1)
                for j in range(jobs):
                    g, half = j // 2, j % 2
                    rows = slice(g * NST, (g + 1) * NST)
                    wait(pe, ko_ready, k, jobs, j + 1 - jobs)
                    for h in range(8):
                        for r in range(2):
                            last = nc.tensor.matmul(psum[3 + j][:, h * STEP:(h + 1) * STEP],
                                                    cp[par][rows, r, half * 8 + h, :],
                                                    qp[par][rows, r, half * 8 + h, :],
                                                    start=(r == 0), stop=(r == 1))
                    last.then_inc(mm_done, 1)

            product(At(0))
            product(At(1))
            with pe.Fori(0, chunks // 2 - 1) as k2:
                product(At(2, k2, 2))
                product(At(3, k2, 2))

        @block.vector
        def _(dve):
            count = [0]

            def link(ins):
                count[0] += 1
                ins.then_inc(dve_step, 1)
                dve.wait_ge(dve_step, count[0])

            def tt(out, a, b, op):
                return nc.vector.tensor_tensor(out, a, b, op)

            def go(ins):
                count[0] += 1
                ins.then_inc(dve_step, 1)

            def settle():
                dve.wait_ge(dve_step, count[0])

            def cmul(o, a, b):
                for i, (p, q) in enumerate(((0, 0), (1, 1), (0, 1), (1, 0))):
                    go(tt(scratch[i], a[p], b[q], ALU.mult))
                settle()
                go(tt(o[0], scratch[0], scratch[1], ALU.subtract))
                go(tt(o[1], scratch[2], scratch[3], ALU.add))
                settle()

            def csquare(o, a, final=None):
                go(tt(scratch[0], a[0], a[0], ALU.mult))
                go(tt(scratch[1], a[1], a[1], ALU.mult))
                go(nc.vector.scalar_tensor_tensor(o[1], a[0], 2.0, a[1], ALU.mult, ALU.mult))
                settle()
                last = tt(o[0], scratch[0], scratch[1], ALU.subtract)
                if final is None:
                    link(last)
                else:
                    last.then_inc(final, 1)
                    dve.wait_ge(final, 1)

            dve.wait_ge(params_in, 80)
            dve.wait_ge(dt_ready, 1)
            dve.wait_ge(exp_ready, 1)
            dtb = dt[:, :].unsqueeze(2).to_broadcast([P, 2, NST])
            f = lambda t: t[:, :, :].rearrange("p g n -> p (g n)")
            link(tt(half_im[:, :, :], aim[:, :, :], dtb, ALU.mult))
            link(nc.vector.tensor_scalar(half_im[:, :, :], half_im[:, :, :], 0.5, None, ALU.mult))
            link(tt(half_re[:, :, :], half_re[:, :, :], dtb, ALU.mult))
            link(nc.vector.tensor_scalar(half_re[:, :, :], half_re[:, :, :], -0.5, None, ALU.mult))
            link(tt(t2[:, :], f(half_im), f(half_im), ALU.mult))
            link(nc.vector.tensor_scalar(t0[:, :], f(half_re), -1.0, 1.0, ALU.mult, ALU.add))
            link(tt(t1[:, :], t0[:, :], t0[:, :], ALU.mult))
            link(tt(t1[:, :], t1[:, :], t2[:, :], ALU.add))
            link(nc.vector.reciprocal(t1[:, :], t1[:, :]))
            link(nc.vector.scalar_tensor_tensor(t0[:, :], f(half_re), 1.0, t0[:, :], ALU.add, ALU.mult))
            link(tt(t0[:, :], t0[:, :], t2[:, :], ALU.subtract))
            link(tt(nat[:, 0, :], t0[:, :], t1[:, :], ALU.mult))
            link(nc.vector.scalar_tensor_tensor(nat[:, 1, :], f(half_im), 2.0, t1[:, :], ALU.mult, ALU.mult))
            bv = bri[:, :, :, :].rearrange("p g n r -> p r (g n)")
            link(nc.vector.tensor_copy(nat[:, 2, :], bv[:, 0, :]))
            nc.vector.tensor_copy(nat[:, 3, :], bv[:, 1, :]).then_inc(nat_ready, 1)
            dve.wait_ge(nat_t, 4)
            link(nc.vector.tensor_copy(pw[:, 0, :, :], psum[0][:, 0:2 * P].rearrange("p (r h) -> p r h", r=2)))
            bt = [t1[:, :], t2[:, :]]
            for r in range(2):
                link(nc.vector.tensor_scalar(bt[r], psum[0][:, (2 + r) * P:(3 + r) * P], 2.0, None, ALU.mult))
            scratch = [t0[:, :], f(half_re), f(half_im), f(aim)]
            steps = [pw[:, i] for i in range(6)] + [big[:, 0], big[:, 1]]
            for i in range(1, 8):
                a = (steps[i - 1][:, 0, :], steps[i - 1][:, 1, :])
                csquare((steps[i][:, 0, :], steps[i][:, 1, :]), a, powers_ready if i == 5 else None)
            d64 = (big[:, 0, 0, :], big[:, 0, 1, :])
            d128 = (big[:, 1, 0, :], big[:, 1, 1, :])
            d192 = (big[:, 2, 0, :], big[:, 2, 1, :])
            cmul(d192, d64, d128)
            for r in range(2):
                link(nc.vector.tensor_copy(bp[:, r, :, 0], bt[r]))
            for a, d in ((1, d64), (2, d128), (3, d192)):
                cmul((bp[:, 0, :, a], bp[:, 1, :, a]), bt, d)
            link(nc.vector.tensor_scalar(bp[:, 2:4, :, :], bp[:, 0:2, :, :], -1.0, None, ALU.mult))
            done = count[0]
            dve.wait_ge(c_copied, 16)

            def stationary(k):
                par = k.parity
                hs = bass.ds(k.times(CHUNK), CHUNK)
                full = [P, CHUNK, HALVES, NC]
                c = [ct[:, r, hs, :].unsqueeze(2).to_broadcast(full) for r in range(2)]
                w = [bp[:, i, hs, :].unsqueeze(3).to_broadcast(full) for i in range(4)]
                pv = [t[:, :].rearrange("p (h a c) -> p h a c", h=CHUNK, a=HALVES) for t in prod]
                o = [cp[par][:, r, :, :].rearrange("p h (a c) -> p h a c", a=HALVES) for r in range(2)]
                wait(dve, mm_done, k, jobs, -jobs)
                tt(pv[0], c[0], w[0], ALU.mult).then_inc(dve_step, 1)
                tt(pv[1], c[1], w[1], ALU.mult).then_inc(dve_step, 1)
                wait(dve, dve_step, k, 4, done + 2)
                tt(o[0], pv[0], pv[1], ALU.subtract).then_inc(cp_re_ready, 1)
                wait(dve, cp_re_ready, k, 1, 1)
                tt(pv[0], c[0], w[3], ALU.mult).then_inc(dve_step, 1)
                tt(pv[1], c[1], w[2], ALU.mult).then_inc(dve_step, 1)
                wait(dve, dve_step, k, 4, done + 4)
                tt(o[1], pv[0], pv[1], ALU.add).then_inc(cp_ready, 1)
                wait(dve, cp_ready, k, 1, 1)

            stationary(At(0))
            stationary(At(1))
            split_weights(nc, dve, wt)
            with dve.Fori(0, chunks // 2 - 1) as k2:
                stationary(At(2, k2, 2))
                stationary(At(3, k2, 2))

        @block.gpsimd
        def _(pool):
            pool.memset(e_const[:, :], 2.718281828459045).then_inc(pool_step, 1)
            pool.wait_ge(params_in, 80)
            pool.wait_ge(pool_step, 1)
            pool.tensor_tensor(dt[:, :], e_const[:, :], dt_in[:, :], ALU.pow).then_inc(dt_ready, 1)
            for par in range(2):
                pool.memset(qp[par][:, 0, :, 0:1], 1.0).then_inc(pool_step, 1)
                pool.memset(qp[par][:, 1, :, 0:1], 0.0).then_inc(pool_step, 1)
            pool.wait_ge(pool_step, 5)
            pool.wait_ge(powers_ready, 1)
            first, per = 5, 2 + 5 * 6 - 1

            def moving(k):
                q = qp[k.parity]
                hs = bass.ds(k.times(CHUNK), CHUNK)
                wait(pool, mm_done, k, jobs, -jobs)
                pool.tensor_copy(qd[:, :, :], pw[:, :, :, hs].rearrange("p i r h -> p (i r) h")).then_inc(pool_step, 1)
                pool.tensor_copy(q[:, :, :, 1:2], pw[:, 0, :, hs].unsqueeze(3)).then_inc(pool_step, 1)
                n = 2
                wait(pool, pool_step, k, per, first + n)
                for i in range(1, 6):
                    m = 1 << i
                    d = [qd[:, 2 * i + r, :].unsqueeze(2).to_broadcast([P, CHUNK, m]) for r in range(2)]
                    s = [q[:, r, :, 0:m] for r in range(2)]
                    u = [t[:, 0:CHUNK * m].rearrange("p (h b) -> p h b", h=CHUNK) for t in qt]
                    pool.tensor_tensor(u[0], s[0], d[0], ALU.mult).then_inc(pool_step, 1)
                    pool.tensor_tensor(u[1], s[1], d[1], ALU.mult).then_inc(pool_step, 1)
                    wait(pool, pool_step, k, per, first + n + 2)
                    pool.tensor_tensor(q[:, 0, :, m:2 * m], u[0], u[1], ALU.subtract).then_inc(pool_step, 1)
                    wait(pool, pool_step, k, per, first + n + 3)
                    pool.tensor_tensor(u[0], s[0], d[1], ALU.mult).then_inc(pool_step, 1)
                    pool.tensor_tensor(u[1], s[1], d[0], ALU.mult).then_inc(pool_step, 1)
                    wait(pool, pool_step, k, per, first + n + 5)
                    last = pool.tensor_tensor(q[:, 1, :, m:2 * m], u[0], u[1], ALU.add)
                    if i < 5:
                        last.then_inc(pool_step, 1)
                        wait(pool, pool_step, k, per, first + n + 6)
                        n += 6
                    else:
                        last.then_inc(qp_ready, 1)
                        wait(pool, qp_ready, k, 1, 1)
                assert n + 5 == per, n

            moving(At(0))
            moving(At(1))
            largest_over_partitions(pool, wt)
            with pool.Fori(0, chunks // 2 - 1) as k2:
                moving(At(2, k2, 2))
                moving(At(3, k2, 2))



class Weights:

    def __init__(self, nc, ctx):
        def sb(name, shape, dtype=F32):
            return ctx.enter_context(nc.sbuf_tensor(name, shape, dtype))

        self.w16 = [sb(f"w16_{i}", [P, LC, UC], F16) for i in range(2)]
        self.scale = sb("scale", [P, 3])
        self.unscale = sb("unscale", [P, 2])
        self.rms_scale = sb("rms_scale", [P, 2])
        self.w = sb("w", [P, LC, WCOLS])
        self.w_in = sb("w_in", [P, LC, 2 * M])
        self.w_out = sb("w_out", [P, TT, DIM])
        self.b_out = sb("b_out", [P, DIM])
        self.ln_w = sb("ln_w", [P, DIM])
        self.ln_b = sb("ln_b", [P, DIM])
        self.w1 = sb("w1", [P, MI])
        self.b1 = sb("b1", [P, MI])
        self.w2 = sb("w2", [P, MI])
        self.b_in = sb("b_in", [P, 1])
        self.b2 = sb("b2", [P, 1])
        self.cls = sb("cls", [P, DIM])
        self.gam = sb("gam", [P, PAIRS])
        self.z = sb("z_cls", [HEADS, DIM])
        self.scc = sb("scc", [HEADS, 1])
        self.mag = sb("mag", [P, 4])
        self.mags = sb("mags", [P, 4])
        self.loaded, self.mag_ready, self.mags_ready, self.split_step = (
            ctx.enter_context(nc.semaphore(n)) for n in ("loaded", "mag_ready", "mags_ready", "split_step"))
        self.half = sb("half", [P, 2 * HEADS])

    def allocate_rest(self, nc, ctx):
        self.wo = ctx.enter_context(nc.sbuf_tensor("wo", [P, PAIRS, DIM], F32))
        self.v_cls = ctx.enter_context(nc.sbuf_tensor("v_cls", [P, INNER], F32))


def load_weights(sp, wt, cls_tok, ln_w, ln_b, wq, wkv, w_in, b_in, w1, b1, w2, b2, w_out, b_out):
    n = 0

    def load(dst, src):
        nonlocal n
        n += 1
        sp.dma_start(dst, src).then_inc(wt.loaded, 16)

    load(wt.w[:, :, QC:QC + INNER], wq.rearrange("(c p) n -> p c n", p=P))
    load(wt.w[:, :, KC:KC + 2 * INNER], wkv.rearrange("(c p) n -> p c n", p=P))
    load(wt.cls[:, :], cls_tok[0, 0, :].partition_broadcast(P))
    load(wt.ln_w[:, :], ln_w.partition_broadcast(P))
    load(wt.ln_b[:, :], ln_b.partition_broadcast(P))
    load(wt.b_out[:, :], b_out.partition_broadcast(P))
    for i in range(2):
        rows = slice(i * M, (i + 1) * M)
        load(wt.w_in[:, :, rows], w_in.rearrange("(c p) m -> p c m", p=P))
        load(wt.w_out[rows, i, :], w_out)
        load(wt.w1[rows, :], w1)
        load(wt.b1[rows, :], b1)
        load(wt.w2[rows, :], w2)
        load(wt.b_in[rows, :], b_in.unsqueeze(1))
        load(wt.b2[rows, :], b2.unsqueeze(1))
    assert n == LOADS, n


def largest_over_partitions(pool, wt):
    pool.wait_ge(wt.mag_ready, 1)
    pool.partition_all_reduce(wt.mags[:, :], wt.mag[:, :], P, RMAX).then_inc(wt.mags_ready, 1)
    pool.wait_ge(wt.mags_ready, 1)


def split_weights(nc, dve, wt):
    count = [0]

    def link(ins):
        count[0] += 1
        ins.then_inc(wt.split_step, 1)
        dve.wait_ge(wt.split_step, count[0])

    tt, ts = nc.vector.tensor_tensor, nc.vector.tensor_scalar
    mag, mags = wt.mag, wt.mags

    def magnitude(col, ap, axis):
        return nc.vector.tensor_reduce(mag[:, col:col + 1], ap, axis, ALU.max, apply_absolute_value=True)

    dve.wait_ge(wt.loaded, 16 * LOADS)
    link(magnitude(0, wt.w[:, :, QC:QC + INNER], AX.XY))
    link(magnitude(1, wt.w[:, :, KC:KC + 2 * INNER], AX.XY))
    link(magnitude(2, wt.ln_w[:, :], AX.X))
    magnitude(3, wt.ln_b[:, :], AX.X).then_inc(wt.mag_ready, 1)
    dve.wait_ge(wt.mags_ready, 1)
    link(tt(mags[:, 2:3], mags[:, 2:3], mags[:, 3:4], ALU.max))
    link(ts(mags[:, 0:3], mags[:, 0:3], 2.0 ** -40, None, ALU.max))
    bits = mags[:, 0:3].bitcast(I32)
    link(ts(bits, bits, 0x7F800000, None, ALU.bitwise_and))
    link(nc.vector.reciprocal(wt.scale[:, :], mags[:, 0:3]))
    link(ts(wt.scale[:, :], wt.scale[:, :], 0.5, None, ALU.mult))
    link(ts(wt.unscale[:, :], mags[:, 0:2], mags[:, 2:3], 4.0, ALU.mult, ALU.mult))
    link(tt(wt.rms_scale[:, 0:1], wt.unscale[:, 1:2], wt.unscale[:, 1:2], ALU.mult))
    link(tt(wt.rms_scale[:, 1:2], wt.unscale[:, 0:1], wt.unscale[:, 0:1], ALU.mult))
    link(ts(wt.rms_scale[:, :], wt.rms_scale[:, :], 1.0 / DH, None, ALU.mult))
    for i, cols in enumerate((slice(QC, QC + INNER), slice(KC, KC + 2 * INNER))):
        hi, lo = (t[:, :, cols] for t in wt.w16)
        link(ts(hi, wt.w[:, :, cols], wt.scale[:, i:i + 1], None, ALU.mult))
        link(nc.vector.scalar_tensor_tensor(lo, wt.w[:, :, cols], wt.scale[:, i:i + 1], hi,
                                            ALU.mult, ALU.subtract))


def class_program(nc, psum, ident, wt, q_gamma, k_gamma, wo):
    ctx = ExitStack()
    with ctx:
        def sb(name, shape):
            return ctx.enter_context(nc.sbuf_tensor(name, shape, F32))

        def sem(name):
            return ctx.enter_context(nc.semaphore(name))

        stats = sb("c_stats", [P, 6])
        mv = sb("c_mv", [P, 2])
        rstd = sb("c_rstd", [P, 1])
        xn = sb("c_xn", [P, DIM])
        xnt = sb("c_xnt", [P, LC, P])
        gq = sb("c_gq", [P, INNER])
        gk = sb("c_gk", [P, INNER])
        row = [sb(f"c_row{i}", [P, INNER]) for i in range(2)]
        tmp = sb("c_tmp", [P, INNER])
        ss = sb("c_ss", [P, 2, HEADS])
        rr = sb("c_rr", [P, 2, HEADS])
        cc = sb("c_cc", [P, HEADS])
        vb = sb("c_vb", [P, PAIRS, HEADS])

        gammas_loaded, wo_loaded = sem("gammas_loaded"), sem("wo_loaded")
        var_ready = sem("c_var_ready")
        rstd_ready = sem("c_rstd_ready")
        pe_step = sem("c_pe_step")
        dve_step = sem("c_dve_step")
        pool_step = sem("c_pool_step")
        ss_ready = sem("c_ss_ready")
        rr_ready = sem("c_rr_ready")
        xn_ready = sem("c_xn_ready")
        xnt_ready = sem("c_xnt_ready")
        rows_ready = sem("c_rows_ready")
        cc_ready = sem("c_cc_ready")
        vb_ready = sem("c_vb_ready")
        block = ctx.enter_context(nc.Block())

        @block.sync
        def _(sp):
            sp.dma_start(wt.wo[:, :, :], wo.rearrange("(c p) n -> p c n", p=P)).then_inc(wo_loaded, 16)
            for t, gamma in ((gq, q_gamma), (gk, k_gamma)):
                sp.dma_start(t[:, :], gamma.rearrange("h o d -> (h o d)").partition_broadcast(P)).then_inc(gammas_loaded, 16)

        @block.gpsimd
        def _(pool):
            pool.memset(wt.half[:, :], -0.5).then_inc(pool_step, 1)
            pool.wait_ge(pool_step, 1)
            pool.wait_ge(var_ready, 1)
            pool.tensor_tensor(rstd[:, :], mv[:, 1:2], wt.half[:, 0:1], ALU.pow).then_inc(rstd_ready, 1)
            pool.wait_ge(ss_ready, 1)
            pool.tensor_tensor(rr[:, :, :].rearrange("p a h -> p (a h)"),
                               ss[:, :, :].rearrange("p a h -> p (a h)"), wt.half[:, :], ALU.pow).then_inc(rr_ready, 1)

        @block.tensor
        def _(pe):
            pe.wait_ge(xn_ready, 1)
            for c in range(LC):
                nc.tensor.transpose(psum[0][:, c * P:(c + 1) * P], xn[:, c * P:(c + 1) * P],
                                    ident[:, :]).then_inc(pe_step, 1)
            pe.wait_ge(xnt_ready, 1)
            for j in range(6):
                for c in range(LC):
                    last = nc.tensor.matmul(psum[1 + j][:, :], xnt[:, c, :], wt.w[:, c, j * 512:(j + 1) * 512],
                                            start=(c == 0), stop=(c == LC - 1))
                last.then_inc(pe_step, 1)
            pe.wait_ge(rows_ready, 1)
            for src, bank in ((wt.v_cls, (0, 7)), (tmp, (1, 2))):
                for c in range(PAIRS):
                    nc.tensor.transpose(psum[bank[c // 4]][:, (c % 4) * P:(c % 4 + 1) * P],
                                        src[:, c * P:(c + 1) * P], ident[:, :]).then_inc(pe_step, 1)
            pe.wait_ge(cc_ready, 1)
            nc.tensor.transpose(psum[3][0:HEADS, 0:P], cc[:, :], ident[:, :]).then_inc(pe_step, 1)
            pe.wait_ge(vb_ready, 1)
            pe.wait_ge(wo_loaded, 16)
            for c in range(PAIRS):
                last = nc.tensor.matmul(psum[4][0:HEADS, 0:DIM], vb[:, c, :], wt.wo[:, c, :],
                                        start=(c == 0), stop=(c == PAIRS - 1))
            last.then_inc(pe_step, 1)

        @block.vector
        def _(dve):
            count = [0]

            def link(ins):
                count[0] += 1
                ins.then_inc(dve_step, 1)
                dve.wait_ge(dve_step, count[0])

            tt, ts = nc.vector.tensor_tensor, nc.vector.tensor_scalar
            for i in range(TT):
                link(nc.vector.memset(wt.w_out[(1 - i) * M:(2 - i) * M, i, :], 0.0))
            link(nc.vector.bn_stats(stats[:, :], wt.cls[:, :]))
            link(nc.vector.bn_aggr(mv[:, :], stats[:, :]))
            ts(mv[:, 1:2], mv[:, 1:2], 1.0 + LN_EPS, LN_EPS * LN_EPS, ALU.mult, ALU.add).then_inc(var_ready, 1)
            dve.wait_ge(rstd_ready, 1)
            link(ts(xn[:, :], wt.cls[:, :], mv[:, 0:1], rstd[:, 0:1], ALU.subtract, ALU.mult))
            link(tt(xn[:, :], xn[:, :], wt.ln_w[:, :], ALU.mult))
            tt(xn[:, :], xn[:, :], wt.ln_b[:, :], ALU.add).then_inc(xn_ready, 1)
            dve.wait_ge(pe_step, LC)
            nc.vector.tensor_copy(xnt[:, :, :].rearrange("p c t -> p (c t)"), psum[0][:, 0:LC * P]).then_inc(xnt_ready, 1)
            heads = lambda ap: ap.rearrange("p (h d) -> p h d", d=DH)
            for i in range(2):
                dve.wait_ge(pe_step, LC + 2 * i + 2)
                for j in range(2):
                    link(nc.vector.tensor_copy(row[i][:, j * 512:(j + 1) * 512], psum[1 + 2 * i + j][:, :]))
                link(tt(tmp[:, :], row[i][:, :], row[i][:, :], ALU.mult))
                link(nc.vector.tensor_reduce(ss[:, i, :], heads(tmp[:, :]), AX.X, ALU.add))
            ts(ss[:, :, :], ss[:, :, :], 1.0 / DH, RMS_EPS, ALU.mult, ALU.add).then_inc(ss_ready, 1)
            dve.wait_ge(pe_step, LC + 6)
            for j in range(2):
                link(nc.vector.tensor_copy(wt.v_cls[:, j * 512:(j + 1) * 512], psum[5 + j][:, :]))
            dve.wait_ge(gammas_loaded, 32)
            link(tt(tmp[:, :], gq[:, :], gk[:, :], ALU.mult))
            ts(tmp[:, :], tmp[:, :], float(DH), None, ALU.mult).then_inc(rows_ready, 1)
            dve.wait_ge(rows_ready, 1)
            dve.wait_ge(rr_ready, 1)
            rb = [rr[:, i, :].unsqueeze(2).to_broadcast([P, HEADS, DH]) for i in range(2)]
            link(tt(heads(row[1][:, :]), heads(row[1][:, :]), rb[1], ALU.mult))
            link(tt(heads(row[0][:, :]), heads(row[0][:, :]), rb[0], ALU.mult))
            link(tt(row[0][:, :], row[0][:, :], tmp[:, :], ALU.mult))
            link(tt(gq[:, :], row[0][:, :], row[1][:, :], ALU.mult))
            nc.vector.tensor_reduce(cc[:, :], heads(gq[:, :]), AX.X, ALU.add).then_inc(cc_ready, 1)
            link(tt(row[1][:, :], row[1][:, :], tmp[:, :], ALU.mult))
            link(nc.vector.memset(vb[:, :, :], 0.0))
            dve.wait_ge(pe_step, LC + 6 + 2 * PAIRS)
            flat = vb[:, :, :].rearrange("p c h -> p (c h)")
            for half in range(2):
                bank = psum[(0, 7)[half]][:, :].rearrange("p (c t) -> p c t", t=P)
                gbank = psum[(1, 2)[half]][:, :].rearrange("p (c t) -> p c t", t=P)
                link(nc.vector.tensor_copy(wt.gam[:, 4 * half:4 * half + 4], gbank[:, :, 0]))
                for i in range(2):
                    rows = slice(i * DH, (i + 1) * DH)
                    lo = 4 * half * (HEADS + 2) + i
                    last = nc.vector.tensor_copy(flat[rows, lo:lo + 3 * (HEADS + 2) + 1:HEADS + 2], bank[rows, :, 0])
                    if half and i:
                        last.then_inc(vb_ready, 1)
                    else:
                        link(last)
            dve.wait_ge(cc_ready, 1)
            for i, (base, r) in enumerate(((KC, row[0]), (QC, row[1]))):
                for c in range(LC):
                    link(tt(gq[:, :], wt.w[:, c, base:base + INNER], r[:, :], ALU.mult))
                    link(nc.vector.tensor_reduce(wt.w[:, c, UC + i * HEADS:UC + (i + 1) * HEADS],
                                                 heads(gq[:, :]), AX.X, ALU.add))
            dve.wait_ge(pe_step, LC + 6 + 2 * PAIRS + 1)
            link(nc.vector.tensor_copy(wt.scc[:, :], psum[3][0:HEADS, 0:1]))
            dve.wait_ge(pe_step, LC + 6 + 2 * PAIRS + 2)
            link(nc.vector.tensor_copy(wt.z[:, :], psum[4][0:HEADS, 0:DIM]))
            link(ts(wt.wo[:, :, :], wt.wo[:, :, :], wt.unscale[:, 1:2], None, ALU.mult))
            link(ts(wt.gam[:, :], wt.gam[:, :], wt.unscale[:, 1:2], 1.0 / DH, ALU.mult, ALU.mult))


LOADS = 6 + 2 * 7



FRONT = [("xt", -3, "dve"), ("k00", -1, "act"), ("k01", -1, "act"), ("k10", 0, "act"),
         ("k11", 0, "act"), ("q00", 1, "act"), ("u", 1, "dve"), ("q01", 2, "act"),
         ("v00", 4, "dve"), ("q10", 4, "act"), ("v01", 5, "dve"), ("qt0", 5, "dve"),
         ("lc", 6, "act"), ("kt0", 7, "dve"), ("kt1", 7, "dve"), ("qt1", 8, "dve"),
         ("q11", 8, "act"), ("pc", 9, "dve"), ("v10", 9, "dve"), ("kt2", 10, "dve"),
         ("v11", 10, "dve"), ("kt3", 11, "dve"), ("qt2", 11, "dve"), ("qt3", 12, "dve"),
         ("xb", 12, "dve")]
SUM_SLOTS = (-1, 0, 0, 1, 1, 3, 5, 9)
RK_SLOT, RQ_SLOT = 2, 11
SCALE_SLOTS = (4, 5)
LC_SLOT = 6
PRE_SLOT = 1
WO_SLOTS = (6, 7, 8)
NORM2_SLOT = 9
GATE_SLOTS = {12: range(0, 3), 13: range(3, 6), 14: range(6, 13), 15: range(13, 16)}
EARLY = 3
SPLIT = [n for n, _, _ in FRONT if n[0] == "v" or n[:2] in ("kt", "qt")]
HIGH_COUNT, HIGH_PARTS = {}, 0
for _n in SPLIT:
    HIGH_PARTS += 2 if _n[0] == "k" else 1
    HIGH_COUNT[_n] = HIGH_PARTS
PARTS = ((0, 0), (0, 1), (1, 0))
EXP_BUFS, PART_BUFS = 2, 4
EXP_LAG, PT_LAG, AV_LAG = 1, 3, 4
BACK = [("ot0", 2, "act"), ("ot1", 2, "act"), ("ot2", 3, "act"), ("ot3", 4, "act"),
        ("pt", 5, "dve"), ("wo", 8, "dve"), ("z2t", 10, "dve"), ("s", 11, "act"),
        ("y", 1, "dve")]


class Jobs:

    def __init__(self, table, banks, ready, freed):
        self.table, self.banks, self.ready, self.freed = table, banks, ready, freed
        self.slot = {name: slot for name, slot, _ in table}
        self.engine = {name: e for name, _, e in table}
        self.at = {name: i for i, (name, _, _) in enumerate(table)}
        self.count = {e: sum(x[2] == e for x in table) for e in ("act", "dve")}

    def in_slot(self, slot, engine=None):
        return [n for n, s, e in self.table if s == slot and (engine is None or e == engine)]

    def bank(self, name):
        return self.banks[self.at[name] % len(self.banks)]

    def wait_ready(self, eng, b, name):
        wait(eng, self.ready, b, len(self.table), self.at[name] + 1)

    def wait_copied(self, eng, b, name):
        i = self.at[name]
        e = self.table[i][2]
        wait(eng, self.freed[e], b, self.count[e], sum(x[2] == e for x in self.table[:i + 1]))

    def wait_bank(self, eng, b, name):
        i = self.at[name] - len(self.banks)
        if len(self.table) % len(self.banks) and i < 0:
            for j in range(len(self.table) - len(self.banks), len(self.table)):
                self.wait_copied(eng, b + -1, self.table[j][0])
            return
        if i < 0:
            self.wait_copied(eng, b + -1, self.table[i][0])
        else:
            self.wait_copied(eng, b, self.table[i][0])


def image_program(nc, psum, ident, ident16, wt, tokens, xb, pcc, out):
    ctx = ExitStack()
    with ctx:
        def sb(name, shape, dtype=F32):
            return ctx.enter_context(nc.sbuf_tensor("i_" + name, shape, dtype))

        def two(name, shape, dtype=F32):
            return [sb(f"{name}{i}", shape, dtype) for i in range(2)]

        def sem(name):
            return ctx.enter_context(nc.semaphore(name))

        x = two("x", [P, TT, DIM])
        carrier = sb("carrier", [P, 1])
        bn = sb("bn", [P, TT, 6])
        mv = sb("mv", [P, TT, 2])
        rstd = sb("rstd", [P, TT])
        xn = two("xn", [P, TT, DIM])
        xnt = sb("xnt", [P, LC, SEQ])
        xnt16 = sb("xnt16", [P, 2, LC, SEQ], F16)
        qs = sb("qs", [P, TT, INNER])
        ks = sb("ks", [P, TT, INNER])
        sq = two("sq", [P, 512])
        ss = sb("ss", [P, 2, TT, HEADS])
        rk = sb("rk", [P, TT, HEADS])
        rq = two("rq", [P, TT, HEADS])
        u = two("u", [P, TT, 2 * HEADS])
        v = two("v", [P, 2, TT, INNER], F16)
        qt = two("qt", [P, 2, PAIRS, SEQ], F16)
        kt = two("kt", [P, 2, PAIRS, SEQ], F16)
        lc = sb("lc", [P, TT, HEADS])
        cm = sb("cm", [HEADS, 1])
        ncm = sb("ncm", [HEADS, 1])
        ce = sb("ce", [HEADS, SEQ])
        cs = sb("cs", [HEADS, 1])
        cse = sb("cse", [HEADS, 1])
        csum = sb("csum", [HEADS, 1])
        cinv = sb("cinv", [HEADS, 1])
        cp = sb("cp", [HEADS, SEQ])
        cpt = sb("cpt", [P, TT, HEADS])
        nrq = sb("nrq", [P, TT, HEADS])
        nru = sb("nru", [P, TT, HEADS])
        scaled = two("scaled", [P, SEQ])
        nb = sb("nb", [P, TT, HEADS])
        e = [sb(f"e{i}", [P, TT, SEQ]) for i in range(EXP_BUFS)]
        e16 = [sb(f"e16_{i}", [P, 2, TT, SEQ], F16) for i in range(PART_BUFS)]
        esum = sb("esum", [P, TT, HEADS])
        earg = sb("earg", [P, TT, HEADS])
        ecls = sb("ecls", [P, TT, HEADS])
        den = sb("den", [P, TT, 4])
        rinv = sb("rinv", [P, TT, HEADS])
        pt = two("pt", [P, 2, TT, SEQ], F16)
        o = sb("o", [P, TT, INNER])
        pcls = sb("pcls", [P, TT, HEADS])
        ot = sb("ot", [P, PAIRS, SEQ])
        pclst = sb("pclst", [HEADS, SEQ])
        xr = sb("xr", [P, TT, DIM])
        h1 = sb("h1", [P, TT, DIM])
        bn2 = sb("bn2", [P, TT, 6])
        mv2 = sb("mv2", [P, TT, 2])
        rstd2 = sb("rstd2", [P, TT])
        yt = sb("yt", [P, LC, SEQ])
        st = sb("st", [P, P])
        relu = [sb(f"relu{i}", [P, P]) for i in range(4)]
        g = two("g", [P, P])
        y = two("y", [P, TT, DIM])

        names = ["var_ready", "rstd_ready", "z_ready", "xn_ready", "front_ready",
                 "front_copied_act", "front_copied_dve", "square_ready", "square_summed", "mean_ready", "rk_ready",
                 "rq_ready", "kn_ready", "lc_ready", "cmax_ready", "cse_ready", "cp_ready",
                 "pool_front_step", "front_step", "pre_step", "scores_ready", "nbias_ready", "exp_done",
                 "ehi_ready", "elo_ready", "xhi_ready", "arg_ready",
                 "ecls_ready", "pt_ready", "pt_copied", "av_done", "o_copied", "attn_step", "pcls_ready",
                 "back_ready", "back_copied_act", "back_copied_dve", "var2_ready", "rstd2_ready",
                 "z2_ready", "hb_ready", "relu_ready", "gate_summed", "gates_ready", "back_step",
                 "group_step",]
        s = {n: sem("i_" + n) for n in names}
        x_loaded, xr_loaded, stored = ([sem(f"i_{n}{p}") for p in range(2)] for n in ("x_loaded", "xr_loaded", "stored"))
        front = Jobs(FRONT, [psum[5], psum[6]], s["front_ready"],
                     {"act": s["front_copied_act"], "dve": s["front_copied_dve"]})
        back = Jobs(BACK, [psum[7]], s["back_ready"],
                    {"act": s["back_copied_act"], "dve": s["back_copied_dve"]})
        heads = lambda ap: ap.rearrange("p (h d) -> p h d", d=DH)

        nothing = lambda b, slot: None

        def images(eng, attention, frontwork, backwork, prework=nothing, late_back=nothing, tail=nothing):
            def slots(b, with_pre=True, with_front=True, with_back=True, with_tail=True):
                for slot in range(HEADS):
                    attention(b, slot)
                    if with_tail:
                        tail(b + -2, slot)
                    if with_back:
                        backwork(b + -1, slot)
                    if with_front:
                        frontwork(b + 1, slot)
                    if with_pre and slot >= HEADS - EARLY:
                        frontwork(b + 2, slot - HEADS)
                    if with_back:
                        late_back(b + -1, slot)
                    if with_pre:
                        prework(b + 2, slot)

            for slot in range(HEADS):
                prework(At(0), slot)
            for slot in range(HEADS):
                frontwork(At(0), slot - EARLY)
                prework(At(1), slot)
            for slot in range(-EARLY, 0):
                frontwork(At(1), slot)
            slots(At(0), with_back=False, with_tail=False)
            slots(At(1), with_tail=False)
            slots(At(2))
            if BATCHES > 6:
                with eng.Fori(0, BATCHES // 2 - 3) as i:
                    slots(At(3, i, 2))
                    slots(At(4, i, 2))
            slots(At(BATCHES - 3))
            slots(At(BATCHES - 2), with_pre=False)
            slots(At(BATCHES - 1), with_pre=False, with_front=False)
            for slot in range(HEADS):
                if slot < AV_LAG:
                    attention(At(BATCHES), slot, last=True)
                tail(At(BATCHES - 2), slot)
                backwork(At(BATCHES - 1), slot)
                late_back(At(BATCHES - 1), slot)
            tail(At(BATCHES - 1), back.slot["y"])

        block = ctx.enter_context(nc.Block())

        @block.sync
        def _(sp):
            def load(b):
                wait(sp, s["z_ready"], b, TT, -TT)
                sp.dma_start(x[b.parity][:, :, :],
                             tokens[bass.ds(b.times(1), 1), :, :].rearrange("b (t p) l -> p (b t) l", p=P)
                             ).then_inc(x_loaded[b.parity], 16)

            def load_residual(b):
                back.wait_copied(sp, b + -1, "wo")
                sp.dma_start(xr[:, :, :],
                             tokens[bass.ds(b.times(1), 1), :, :].rearrange("b (t p) l -> p (b t) l", p=P)
                             ).then_inc(xr_loaded[b.parity], 16)

            def store(b):
                back.wait_copied(sp, b, "y")
                sp.dma_start(out[bass.ds(b.times(1), 1), 1:, :].rearrange("b (t p) l -> p (b t) l", p=P),
                             y[b.parity][:, :, :]).then_inc(stored[b.parity], 16)

            def steady(b):
                load(b)
                store(b + -4)
                load_residual(b + -2)

            load(At(0))
            load(At(1))
            load_residual(At(0))
            load(At(2))
            load(At(3))
            load_residual(At(1))
            if BATCHES > 6:
                with sp.Fori(0, BATCHES // 2 - 3) as i:
                    steady(At(4, i, 2))
                    steady(At(5, i, 2))
            steady(At(BATCHES - 2))
            steady(At(BATCHES - 1))
            for b in range(BATCHES - 4, BATCHES):
                store(At(b))
                if b < BATCHES - 2:
                    load_residual(At(b + 2))
            for p in range(2):
                sp.wait_ge(stored[p], 16 * (BATCHES // 2))

        @block.gpsimd
        def _(pool):
            step = Steps(pool, s["pool_front_step"], 12)

            def half_power(dst, src, ready):
                pool.tensor_tensor(dst, src, wt.half[:, 0:dst.shape[1]], ALU.pow).then_inc(ready, 1)

            def scale_keys(b, half, t):
                cols = slice(half * 512, half * 512 + 512)
                kv = heads(ks[:, t, cols])
                pool.tensor_tensor(kv, kv, rk[:, t, half * 8:half * 8 + 8].unsqueeze(2).to_broadcast([P, 8, DH]),
                                   ALU.mult).then_inc(s["kn_ready"], 1)

            def pre_work(b, slot):
                if slot == PRE_SLOT:
                    step.begin(b)
                    wait(pool, s["var_ready"], b, 1, 1)
                    half_power(rstd[:, :], mv[:, :, 1], s["rstd_ready"])
                if slot == PRE_SLOT + 2:
                    wait(pool, s["z_ready"], b, TT, TT)
                    wn, bnn = (t[:, :].unsqueeze(1).to_broadcast([P, TT, DIM]) for t in (wt.ln_w, wt.ln_b))
                    xv = xn[b.parity][:, :, :]
                    step.did(pool.tensor_tensor(xv, xv, wn, ALU.mult))
                    step.settle()
                    pool.tensor_tensor(xv, xv, bnn, ALU.add).then_inc(s["xn_ready"], 1)

            def front_work(b, slot):
                if slot == RK_SLOT:
                    wait(pool, s["mean_ready"], b, 2, 1)
                    half_power(rk[:, :, :].rearrange("p t h -> p (t h)"),
                               ss[:, 0, :, :].rearrange("p t h -> p (t h)"), s["rk_ready"])
                if slot in SCALE_SLOTS:
                    if slot == SCALE_SLOTS[0]:
                        front.wait_copied(pool, b, "k11")
                        wait(pool, s["rk_ready"], b, 1, 1)
                    for t in range(TT):
                        scale_keys(b, slot - SCALE_SLOTS[0], t)
                if slot == RQ_SLOT:
                    wait(pool, s["mean_ready"], b, 2, 2)
                    half_power(rq[b.parity][:, :, :].rearrange("p t h -> p (t h)"),
                               ss[:, 1, :, :].rearrange("p t h -> p (t h)"), s["rq_ready"])

            def back_work(b, slot):
                if slot == NORM2_SLOT - 1:
                    wait(pool, s["var2_ready"], b, 1, 1)
                    half_power(rstd2[:, :], mv2[:, :, 1], s["rstd2_ready"])
                if slot == NORM2_SLOT - 1:
                    wait(pool, stored[b.parity], b.half, 16, 0)
                    pool.tensor_tensor(y[b.parity][:, :, :], h1[:, :, :], wt.b_out[:, :].unsqueeze(1).to_broadcast([P, TT, DIM]),
                                       ALU.add).then_inc(s["hb_ready"], 1)

            def attention(b, slot, last=False):
                if slot >= EXP_LAG:
                    if not last:
                        low_probs(b, slot - EXP_LAG)
                elif b.reg is not None or b.add > 0:
                    low_probs(b + -1, HEADS + slot - EXP_LAG)

            def low_probs(b, h):
                wait(pool, s["ehi_ready"], b, HEADS, h + 1)
                wait(pool, s["pt_ready"], b, HEADS, h + 1 - PART_BUFS)
                hi, lo = (e16[h % PART_BUFS][:, i, :, :].rearrange("p t k -> p (t k)") for i in range(2))
                pool.tensor_tensor(lo, e[h % EXP_BUFS][:, :, :].rearrange("p t k -> p (t k)"), hi,
                                   ALU.subtract).then_inc(s["elo_ready"], 1)

            step.per = 1
            images(pool, attention, front_work, back_work, pre_work)

        @block.tensor
        def _(pe):
            mm, tr = nc.tensor.matmul, nc.tensor.transpose

            def scores(b, h):
                par, pair, rows = b.parity, h // 2, slice((h % 2) * DH, (h % 2 + 1) * DH)
                if h == 0:
                    front.wait_copied(pe, b, "qt3")
                    front.wait_copied(pe, b, "kt3")
                wait(pe, s["exp_done"], b, 2 * HEADS, 2 * (h - 1))
                for t in range(TT):
                    for n, (i, j) in enumerate(PARTS):
                        last = mm(psum[h % 2][:, t * SEQ:(t + 1) * SEQ], qt[par][rows, i, pair, t * P:(t + 1) * P],
                                  kt[par][rows, j, pair, :], start=(n == 0), stop=(n == 2))
                last.then_inc(s["scores_ready"], 1)

            def transpose_probs(b, h):
                wait(pe, s["elo_ready"], b, HEADS, h + 1)
                wait(pe, s["pt_copied"], b, HEADS, h - 1)
                bank = psum[2 + h % 2][:, :].bitcast(F16)
                for i in range(2):
                    for k in range(TT):
                        for t in range(TT):
                            lo = ((i * TT + k) * TT + t) * P
                            last = tr(bank[:, lo:lo + P], e16[h % PART_BUFS][:, i, t, k * P:(k + 1) * P], ident16[:, :])
                last.then_inc(s["pt_ready"], 1)

            def values(b, h):
                wait(pe, s["pt_copied"], b, HEADS, h + 1)
                if h % 4 == 0:
                    wait(pe, s["o_copied"], b, GROUPS, h // 4)
                for t in range(TT):
                    for n, (i, j, k) in enumerate((i, j, k) for k in range(TT) for i, j in PARTS):
                        lo = (t * 4 + h % 4) * DH
                        last = mm(psum[4][:, lo:lo + DH], pt[h % 2][:, i, k, t * P:(t + 1) * P],
                                  v[b.parity][:, j, k, h * DH:(h + 1) * DH], start=(n == 0), stop=(n == 5))
                last.then_inc(s["av_done"], 1)

            def attention(b, slot, last=False):
                if not last:
                    scores(b, slot)
                for work, lag in ((transpose_probs, PT_LAG), (values, AV_LAG)):
                    if slot >= lag:
                        if not last:
                            work(b, slot - lag)
                    elif b.reg is not None or b.add > 0:
                        work(b + -1, HEADS + slot - lag)

            def front_job(b, name):
                par, bank = b.parity, front.bank(name)
                front.wait_bank(pe, b, name)
                if name == "xt":
                    wait(pe, s["xn_ready"], b, 1, 1)
                    for c in range(LC):
                        for t in range(TT):
                            last = tr(bank[:, (c * TT + t) * P:(c * TT + t + 1) * P],
                                      xn[par][:, t, c * P:(c + 1) * P], ident[:, :])
                elif name[0] in "kqv" and name[1] in "01":
                    half, t = int(name[1]), int(name[2])
                    col = {"q": QC, "k": KC, "v": VC}[name[0]] + half * 512
                    if name == "k00":
                        front.wait_copied(pe, b, "xt")
                    for n, (i, j, c) in enumerate((i, j, c) for c in range(LC) for i, j in PARTS):
                        last = mm(bank[:, :], xnt16[:, i, c, t * P:(t + 1) * P], wt.w16[j][:, c, col:col + 512],
                                  start=(n == 0), stop=(n == 5))
                elif name == "u":
                    for t in range(TT):
                        for c in range(LC):
                            last = mm(bank[:, t * 2 * HEADS:(t + 1) * 2 * HEADS], xnt[:, c, t * P:(t + 1) * P],
                                      wt.w[:, c, UC:UC + 2 * HEADS], start=(c == 0), stop=(c == LC - 1))
                elif name[:2] in ("kt", "qt"):
                    j = int(name[2])
                    if name[0] == "k":
                        wait(pe, s["kn_ready"], b, 4, 2 * (j // 2) + 2)
                        src = ks
                    else:
                        front.wait_copied(pe, b, f"q{j // 2}1")
                        src = qs
                    for pr in range(2):
                        for t in range(TT):
                            lo = (2 * j + pr) * P
                            last = tr(bank[:, (pr * TT + t) * P:(pr * TT + t + 1) * P], src[:, t, lo:lo + P],
                                      ident[:, :])
                elif name == "lc":
                    wait(pe, s["lc_ready"], b, 1, 1)
                    for t in range(TT):
                        last = tr(bank[0:HEADS, t * P:(t + 1) * P], lc[:, t, :], ident[:, :])
                elif name == "pc":
                    wait(pe, s["cp_ready"], b, 1, 1)
                    for t in range(TT):
                        last = mm(bank[:, t * HEADS:(t + 1) * HEADS], cp[:, t * P:(t + 1) * P],
                                  ident[0:HEADS, 0:HEADS], start=True, stop=True)
                elif name == "xb":
                    front.wait_copied(pe, b, "pc")
                    for c in range(LC):
                        for t in range(TT):
                            last = mm(bank[:, c * HEADS:(c + 1) * HEADS], xn[par][:, t, c * P:(c + 1) * P],
                                      cpt[:, t, :], start=(t == 0), stop=(t == TT - 1))
                last.then_inc(s["front_ready"], 1)

            def project_output(b, part):
                bank = back.bank("wo")
                if part == 0:
                    back.wait_bank(pe, b, "wo")
                    back.wait_copied(pe, b, "ot3")
                products = [(t, c) for t in range(TT) for c in range(PAIRS + 1)]
                size = len(products) // len(WO_SLOTS)
                for t, c in products[part * size:(part + 1) * size]:
                    dst = bank[:, t * DIM:(t + 1) * DIM]
                    if c < PAIRS:
                        mm(dst, ot[:, c, t * P:(t + 1) * P], wt.wo[:, c, :], start=(c == 0), stop=False)
                    else:
                        last = mm(dst, pclst[:, t * P:(t + 1) * P], wt.z[:, :], start=False, stop=True)
                if part == len(WO_SLOTS) - 1:
                    last.then_inc(s["back_ready"], 1)

            def back_work(b, slot):
                if slot in WO_SLOTS:
                    project_output(b, WO_SLOTS.index(slot))
                for n in back.in_slot(slot):
                    if n not in ("wo", "y"):
                        back_job(b, n)

            def back_job(b, name):
                bank = back.bank(name)
                back.wait_bank(pe, b, name)
                if name[:2] == "ot":
                    j = int(name[2])
                    wait(pe, s["o_copied"], b, GROUPS, j + 1)
                    for pr in range(2):
                        for t in range(TT):
                            lo = (2 * j + pr) * P
                            last = tr(bank[:, (pr * TT + t) * P:(pr * TT + t + 1) * P], o[:, t, lo:lo + P],
                                      ident[:, :])
                elif name == "pt":
                    wait(pe, s["pcls_ready"], b, 1, 1)
                    for t in range(TT):
                        last = tr(bank[0:HEADS, t * P:(t + 1) * P], pcls[:, t, :], ident[:, :])
                elif name == "z2t":
                    wait(pe, s["z2_ready"], b, 1, 1)
                    for c in range(LC):
                        for t in range(TT):
                            last = tr(bank[:, (c * TT + t) * P:(c * TT + t + 1) * P], h1[:, t, c * P:(c + 1) * P],
                                      ident[:, :])
                elif name == "s":
                    for c in range(LC):
                        last = mm(bank[:, 0:SEQ], wt.w_in[:, c, :], yt[:, c, :], start=(c == 0), stop=(c == LC - 1))
                elif name == "y":
                    wait(pe, s["gates_ready"], b, 1, 1)
                    for t in range(TT):
                        last = mm(bank[:, t * DIM:(t + 1) * DIM], g[0][:, :], wt.w_out[:, t, :],
                                  start=True, stop=True)
                last.then_inc(s["back_ready"], 1)

            images(pe, attention,
                   lambda b, slot: [front_job(b, n) for n in front.in_slot(slot)],
                   back_work, tail=lambda b, slot: back_job(b, "y") if slot == back.slot["y"] else None)

        @block.scalar
        def _(act):
            run = nc.scalar.activation

            def exponentials(b, h):
                wait(act, s["nbias_ready"], b, 2 * HEADS, 2 * h + 2)
                wait(act, s["elo_ready"], b, HEADS, h + 1 - EXP_BUFS)
                for t in range(TT):
                    run(e[h % EXP_BUFS][:, t, :], psum[h % 2][:, t * SEQ:(t + 1) * SEQ], ACT.Exp,
                        scale=rq[b.parity][:, t, h:h + 1], bias=nb[:, t, h:h + 1],
                        accum_out=esum[:, t, h:h + 1]).then_inc(s["exp_done"], 1)
                wait(act, s["pt_ready"], b, HEADS, h + 1 - PART_BUFS)
                wait(act, s["exp_done"], b, 2 * HEADS, 2 * (h + 1))
                run(e16[h % PART_BUFS][:, 0, :, :], e[h % EXP_BUFS][:, :, :], ACT.Copy).then_inc(s["ehi_ready"], 1)
                if h % 4 == 3:
                    if h == 3:
                        wait(act, s["pcls_ready"], b + -1, 1, 1)
                    wait(act, s["arg_ready"], b, GROUPS, h // 4 + 1)
                    cols = slice(h - 3, h + 1)
                    run(ecls[:, :, cols], earg[:, :, cols], ACT.Exp).then_inc(s["ecls_ready"], 1)

            def attention(b, slot, last=False):
                if slot >= EXP_LAG:
                    if not last:
                        exponentials(b, slot - EXP_LAG)
                elif b.reg is not None or b.add > 0:
                    exponentials(b + -1, HEADS + slot - EXP_LAG)

            def front_job(b, name):
                par, bank = b.parity, front.bank(name)
                if name[0] == "v" or name[:2] in ("qt", "kt"):
                    front.wait_ready(act, b, name)
                    if name[0] == "v":
                        half, t = int(name[1]), int(name[2])
                        run(v[par][:, 0, t, half * 512:half * 512 + 512], bank[:, :], ACT.Copy).then_inc(s["xhi_ready"], 1)
                    elif name[0] == "q":
                        j = int(name[2])
                        run(qt[par][:, 0, 2 * j:2 * j + 2, :].rearrange("p c t -> p (c t)"), bank[:, :],
                            ACT.Copy).then_inc(s["xhi_ready"], 1)
                    else:
                        for pr in range(2):
                            c = 2 * int(name[2]) + pr
                            run(kt[par][:, 0, c, :], bank[:, pr * SEQ:(pr + 1) * SEQ], ACT.Copy,
                                scale=wt.gam[:, c:c + 1]).then_inc(s["xhi_ready"], 1)
                    return
                front.wait_ready(act, b, name)
                if name[0] in "kqv" and name[1] in "01":
                    half, t = int(name[1]), int(name[2])
                    dst = {"q": qs, "k": ks}[name[0]]
                    n = 4 * (name[0] == "q") + 2 * half + t
                    wait(act, s["square_summed"], b, 8, n - 1)
                    run(sq[n % 2][:, :], bank[:, :], ACT.Square).then_inc(s["square_ready"], 1)
                    ins = run(dst[:, t, half * 512:half * 512 + 512], bank[:, :], ACT.Copy)
                else:
                    wait(act, s["cmax_ready"], b, 1, 1)
                    ins = run(ce[:, :], bank[0:HEADS, 0:SEQ], ACT.Exp, bias=ncm[:, 0:1], accum_out=cs[:, 0:1])
                ins.then_inc(s["front_copied_act"], 1)
                if name == "lc":
                    run(cse[:, :], wt.scc[:, :], ACT.Exp, bias=ncm[:, 0:1]).then_inc(s["cse_ready"], 1)

            def back_job(b, name):
                bank = back.bank(name)
                back.wait_ready(act, b, name)
                if name == "s":
                    for t in range(TT):
                        rows = slice(t * M, (t + 1) * M)
                        ins = run(st[rows, :], bank[rows, t * P:(t + 1) * P], ACT.Identity, bias=wt.b_in[rows, 0:1])
                        if t == 0:
                            ins.then_inc(s["relu_ready"], 1)
                else:
                    j = int(name[2])
                    ins = run(ot[:, 2 * j:2 * j + 2, :].rearrange("p c t -> p (c t)"), bank[:, :], ACT.Copy)
                ins.then_inc(s["back_copied_act"], 1)

            def back_work(b, slot):
                for n in back.in_slot(slot, "act"):
                    back_job(b, n)

            def gates(b, slot):
                if slot in GATE_SLOTS:
                    if 0 in GATE_SLOTS[slot]:
                        back.wait_copied(act, b, "s")
                        wait(act, s["relu_ready"], b, MI + 1, 1)
                    for i in GATE_SLOTS[slot]:
                        wait(act, s["gate_summed"], b, MI + 1, i - 2)
                        run(relu[i % 4][:, :], st[:, :], ACT.Relu, scale=wt.w1[:, i:i + 1],
                            bias=wt.b1[:, i:i + 1]).then_inc(s["relu_ready"], 1)

            images(act, attention,
                   lambda b, slot: [front_job(b, n) for n in front.in_slot(slot)
                                    if front.engine[n] == "act" or n in SPLIT], back_work, late_back=gates)

        @block.vector
        def _(dve):
            tt, ts = nc.vector.tensor_tensor, nc.vector.tensor_scalar
            fs = Steps(dve, s["front_step"], 13)
            bs = Steps(dve, s["back_step"], 4)
            ps = Steps(dve, s["pre_step"], 5)
            at = Steps(dve, s["attn_step"], 40)

            def normalise_stats(src, stats, mean_var, step):
                for t in range(TT):
                    step.did(nc.vector.bn_stats(stats[:, t, :], src[:, t, :]))
                step.settle()
                step.did(nc.vector.memset(carrier[:, :], 0.0))
                for t in range(TT):
                    step.did(nc.vector.bn_aggr(mean_var[:, t, :], stats[:, t, :]))
                step.settle()
                return mean_var[:, :, 1]

            def max_and_bias(b, h):
                wait(dve, s["scores_ready"], b, HEADS, h + 1)
                for t in range(TT):
                    wait(dve, s["nbias_ready"], b, 2 * HEADS, 2 * h + t - 1)
                    ts(scaled[t][:, :], psum[h % 2][:, t * SEQ:(t + 1) * SEQ], nrq[:, t, h:h + 1],
                       nru[:, t, h:h + 1], ALU.mult, ALU.min,
                       accum_out=nb[:, t, h:h + 1]).then_inc(s["nbias_ready"], 1)

            def class_key_argument(b, h):
                if h % 4 == 3:
                    cols = slice(h - 3, h + 1)
                    wait(dve, s["nbias_ready"], b, 2 * HEADS, 2 * h + 2)
                    tt(earg[:, :, cols], nb[:, :, cols], nru[:, :, cols], ALU.subtract).then_inc(s["arg_ready"], 1)

            def copy_probs(b, h):
                wait(dve, s["pt_ready"], b, HEADS, h + 1)
                wait(dve, s["av_done"], b, HEADS, h - 1)
                nc.vector.tensor_copy(pt[h % 2][:, :, :, :].rearrange("p i k q -> p (i k q)"),
                                      psum[2 + h % 2][:, :].bitcast(F16)).then_inc(s["pt_copied"], 1)

            def group_sums(b, q):
                cols = slice(4 * q, 4 * q + 4)
                wait(dve, s["ecls_ready"], b, GROUPS, q + 1)
                tt(den[:, :, :], esum[:, :, cols], ecls[:, :, cols], ALU.add).then_inc(s["group_step"], 1)

            def group_inverses(b, q):
                cols = slice(4 * q, 4 * q + 4)
                wait(dve, s["group_step"], b, 2 * GROUPS, 2 * q + 1)
                nc.vector.reciprocal(rinv[:, :, cols], den[:, :, :]).then_inc(s["group_step"], 1)

            def output_group(b, q):
                cols = slice(4 * q, 4 * q + 4)
                wait(dve, s["group_step"], b, 2 * GROUPS, 2 * q + 2)
                wait(dve, s["av_done"], b, HEADS, 4 * q + 4)
                tt(o[:, :, q * 4 * DH:(q + 1) * 4 * DH].rearrange("p t (h d) -> p t h d", d=DH),
                   psum[4][:, :].rearrange("p (t h d) -> p t h d", t=TT, d=DH),
                   rinv[:, :, cols].unsqueeze(3).to_broadcast([P, TT, 4, DH]), ALU.mult).then_inc(s["o_copied"], 1)

            def attention(b, slot, last=False):
                started = b.reg is not None or b.add > 0
                if slot == 0 and not last:
                    at.begin(b)
                    wait(dve, s["rq_ready"], b, 1, 1)
                    wait(dve, s["arg_ready"], b, GROUPS, 0)
                    at.did(ts(nrq[:, :, :], rq[b.parity][:, :, :], -1.0, None, ALU.mult))
                    at.settle()
                    at.did(tt(nru[:, :, :], nrq[:, :, :], u[b.parity][:, :, HEADS:], ALU.mult))
                    at.settle()
                    at.did(ts(nrq[:, :, :], nrq[:, :, :], wt.unscale[:, 0:1], float(DH), ALU.mult, ALU.mult))
                    at.settle()
                    at.did(ts(rq[b.parity][:, :, :], nrq[:, :, :], -1.0, None, ALU.mult))
                if not last:
                    max_and_bias(b, slot)
                if slot >= PT_LAG:
                    if not last:
                        copy_probs(b, slot - PT_LAG)
                elif started:
                    copy_probs(b + -1, HEADS + slot - PT_LAG)
                if not last:
                    class_key_argument(b, slot)
                for work, at_slot in ((group_sums, AV_LAG - 3), (group_inverses, AV_LAG - 2)):
                    if slot == at_slot and started:
                        work(b + -1, GROUPS - 1)
                    elif slot % 4 == at_slot % 4 and slot > at_slot and not last:
                        work(b, (slot - at_slot - 4) // 4)
                if slot == AV_LAG - 1 and started:
                    output_group(b + -1, GROUPS - 1)
                    tt(pcls[:, :, :], ecls[:, :, :], rinv[:, :, :], ALU.mult).then_inc(s["pcls_ready"], 1)
                elif slot % 4 == (AV_LAG - 1) % 4 and slot > AV_LAG and not last:
                    output_group(b, (slot - AV_LAG - 3) // 4)

            def front_job(b, name):
                par, bank = b.parity, front.bank(name)
                front.wait_ready(dve, b, name)
                if name == "xt":
                    ins = nc.vector.tensor_copy(xnt[:, :, :].rearrange("p c t -> p (c t)"), bank[:, :])
                    fs.did(ins)
                    fs.settle()
                    sx = wt.scale[:, 2:3]
                    fs.did(ts(xnt16[:, 0, :, :], xnt[:, :, :], sx, None, ALU.mult))
                    fs.settle()
                    ins = nc.vector.scalar_tensor_tensor(xnt16[:, 1, :, :], xnt[:, :, :], sx, xnt16[:, 0, :, :],
                                                         ALU.mult, ALU.subtract)
                elif name == "u":
                    ins = nc.vector.tensor_copy(u[par][:, :, :].rearrange("p t h -> p (t h)"), bank[:, 0:TT * 2 * HEADS])
                elif name in SPLIT:
                    wait(dve, s["xhi_ready"], b, HIGH_PARTS, HIGH_COUNT[name])
                    if name[0] == "v":
                        half, t = int(name[1]), int(name[2])
                        hi, lo = (v[par][:, i, t, half * 512:half * 512 + 512] for i in range(2))
                        ins = tt(lo, bank[:, :], hi, ALU.subtract)
                    elif name[0] == "q":
                        j = int(name[2])
                        hi, lo = (qt[par][:, i, 2 * j:2 * j + 2, :].rearrange("p c t -> p (c t)") for i in range(2))
                        ins = tt(lo, bank[:, :], hi, ALU.subtract)
                    else:
                        for pr in range(2):
                            c = 2 * int(name[2]) + pr
                            ins = nc.vector.scalar_tensor_tensor(kt[par][:, 1, c, :], bank[:, pr * SEQ:(pr + 1) * SEQ],
                                                                 wt.gam[:, c:c + 1], kt[par][:, 0, c, :],
                                                                 ALU.mult, ALU.subtract)
                            if pr == 0:
                                fs.did(ins)
                elif name == "pc":
                    ins = nc.vector.tensor_copy(cpt[:, :, :].rearrange("p t h -> p (t h)"), bank[:, 0:TT * HEADS])
                else:
                    ins = nc.vector.tensor_copy(xb[:, bass.ds(b.times(1), 1), :].rearrange("p b n -> p (b n)"),
                                                bank[:, 0:LC * HEADS])
                ins.then_inc(s["front_copied_dve"], 1)

            def pre_work(b, slot):
                par = b.parity
                if slot == PRE_SLOT:
                    ps.begin(b)
                    wait(dve, x_loaded[par], b.half, 16, 16)
                    var = normalise_stats(x[par], bn, mv, ps)
                    ts(var, var, 1.0 + LN_EPS, LN_EPS * LN_EPS, ALU.mult, ALU.add).then_inc(s["var_ready"], 1)
                    ps.end()
                if slot == PRE_SLOT + 1:
                    wait(dve, s["rstd_ready"], b, 1, 1)
                    for t in range(TT):
                        ts(xn[par][:, t, :], x[par][:, t, :], mv[:, t, 0:1], rstd[:, t:t + 1],
                           ALU.subtract, ALU.mult).then_inc(s["z_ready"], 1)

            def front_work(b, slot):
                par = b.parity
                if slot == -EARLY:
                    fs.begin(b)
                fs.b = b
                for n in (n for n in range(8) if SUM_SLOTS[n] == slot):
                    which, half, t = n // 4, n % 4 // 2, n % 2
                    wait(dve, s["square_ready"], b, 8, n + 1)
                    nc.vector.tensor_reduce(ss[:, which, t, half * 8:half * 8 + 8], heads(sq[n % 2][:, :]),
                                            AX.X, ALU.add).then_inc(s["square_summed"], 1)
                    if n % 4 == 3:
                        wait(dve, s["square_summed"], b, 8, n + 1)
                        f = ss[:, which, :, :]
                        ts(f, f, wt.rms_scale[:, which:which + 1], RMS_EPS, ALU.mult, ALU.add).then_inc(s["mean_ready"], 1)
                if slot == LC_SLOT:
                    wait(dve, s["rk_ready"], b, 1, 1)
                    front.wait_copied(dve, b, "u")
                    tt(lc[:, :, :], rk[:, :, :], u[par][:, :, 0:HEADS], ALU.mult).then_inc(s["lc_ready"], 1)
                    front.wait_ready(dve, b, "lc")
                    fs.did(nc.vector.tensor_reduce(cm[:, :], front.bank("lc")[0:HEADS, 0:SEQ], AX.X, ALU.max))
                    fs.settle()
                    ts(ncm[:, :], cm[:, :], wt.scc[:, 0:1], -1.0, ALU.max, ALU.mult).then_inc(s["cmax_ready"], 1)
                if slot == LC_SLOT + 1:
                    wait(dve, s["cse_ready"], b, 1, 1)
                    fs.did(tt(csum[:, :], cs[:, :], cse[:, :], ALU.add))
                    fs.settle()
                    fs.did(nc.vector.reciprocal(cinv[:, :], csum[:, :]))
                    fs.settle()
                    fs.did(tt(pcc[:, bass.ds(b.times(1), 1)], cse[:, :], cinv[:, :], ALU.mult))
                    ts(cp[:, :], ce[:, :], cinv[:, 0:1], None, ALU.mult).then_inc(s["cp_ready"], 1)
                for n in front.in_slot(slot, "dve"):
                    front_job(b, n)
                if slot == HEADS - 1 - EARLY:
                    fs.end()

            def back_work(b, slot):
                if slot == 0:
                    bs.begin(b)
                if slot == back.slot["pt"]:
                    back.wait_ready(dve, b, "pt")
                    nc.vector.tensor_copy(pclst[:, :], psum[7][0:HEADS, 0:SEQ]).then_inc(s["back_copied_dve"], 1)
                if slot == back.slot["wo"]:
                    back.wait_ready(dve, b, "wo")
                    wait(dve, xr_loaded[b.parity], b.half, 16, 16)
                    tt(h1[:, :, :].rearrange("p t l -> p (t l)"), psum[7][:, :],
                       xr[:, :, :].rearrange("p t l -> p (t l)"), ALU.add).then_inc(s["back_copied_dve"], 1)
                    back.wait_copied(dve, b, "wo")
                    var = normalise_stats(h1, bn2, mv2, bs)
                    ts(var, var, LN_EPS, None, ALU.add).then_inc(s["var2_ready"], 1)
                if slot == NORM2_SLOT:
                    wait(dve, s["rstd2_ready"], b, 1, 1)
                    wait(dve, s["hb_ready"], b, 1, 1)
                    for t in range(TT):
                        ts(h1[:, t, :], h1[:, t, :], mv2[:, t, 0:1], rstd2[:, t:t + 1],
                           ALU.subtract, ALU.mult).then_inc(s["gate_summed" if t == 0 else "z2_ready"], 1)
                if slot == back.slot["z2t"]:
                    back.wait_ready(dve, b, "z2t")
                    nc.vector.tensor_copy(yt[:, :, :].rearrange("p c t -> p (c t)"),
                                          psum[7][:, :]).then_inc(s["back_copied_dve"], 1)
                if slot == HEADS - 1:
                    bs.end()

            def tail(b, slot):
                if slot == back.slot["y"]:
                    back.wait_ready(dve, b, "y")
                    wait(dve, s["hb_ready"], b, 1, 1)
                    yv = y[b.parity]
                    tt(yv[:, :, :].rearrange("p t l -> p (t l)"), psum[7][:, :],
                       yv[:, :, :].rearrange("p t l -> p (t l)"), ALU.add).then_inc(s["back_copied_dve"], 1)

            def gates(b, slot):
                if slot in GATE_SLOTS:
                    for i in GATE_SLOTS[slot]:
                        wait(dve, s["relu_ready"], b, MI + 1, i + 2)
                        wait(dve, s["gate_summed"], b, MI + 1, i)
                        acc, term = g[i % 2], relu[i % 4]
                        if i == 0:
                            ins = ts(acc[:, :], term[:, :], wt.w2[:, 0:1], wt.b2[:, 0:1], ALU.mult, ALU.add)
                        elif i == 1:
                            ins = ts(acc[:, :], term[:, :], wt.w2[:, 1:2], None, ALU.mult)
                        else:
                            ins = nc.vector.scalar_tensor_tensor(acc[:, :], term[:, :], wt.w2[:, i:i + 1], acc[:, :],
                                                                 ALU.mult, ALU.add)
                        ins.then_inc(s["gate_summed"], 1)
                    if MI - 1 in GATE_SLOTS[slot]:
                        wait(dve, s["gate_summed"], b, MI + 1, MI + 1)
                        tt(g[0][:, :], g[0][:, :], g[1][:, :], ALU.add).then_inc(s["gates_ready"], 1)

            fs.per, bs.per, at.per, ps.per = 10, 5, 4, 5
            images(dve, attention, front_work, back_work, pre_work, gates, tail)



def class_rows_program(nc, psum, ident, wt, xb, pcc, out):
    B = BATCHES
    ctx = ExitStack()
    with ctx:
        def sb(name, shape):
            return ctx.enter_context(nc.sbuf_tensor("r_" + name, shape, F32))

        def sem(name):
            return ctx.enter_context(nc.semaphore("r_" + name))

        pc = sb("pc", [B, HEADS])
        up = sb("up", [B, 1])
        oc = sb("oc", [B, INNER])
        ot = sb("ot", [P, PAIRS, B])
        h1 = sb("h1", [B, DIM])
        bn = sb("bn", [B, 6])
        mv = sb("mv", [B, 2])
        rstd = sb("rstd", [B, 1])
        z = sb("z", [B, DIM])
        zt = sb("zt", [P, LC, B])
        st = sb("st", [M, B])
        term = sb("term", [M, MI, B])
        g = sb("g", [M, B])
        y = sb("y", [B, DIM])
        pe_step, dve_step, act_step = sem("pe_step"), sem("dve_step"), sem("act_step")
        oc_ready, ot_ready, var_ready, rstd_ready = sem("oc_ready"), sem("ot_ready"), sem("var_ready"), sem("rstd_ready")
        z_ready, zt_ready, g_ready, y_ready, stored = (sem(n) for n in ("z_ready", "zt_ready", "g_ready", "y_ready", "stored"))
        block = ctx.enter_context(nc.Block())

        @block.sync
        def _(sp):
            sp.wait_ge(y_ready, 1)
            sp.dma_start(out[:, 0, :], y[:, :]).then_inc(stored, 16)
            sp.wait_ge(stored, 16)

        @block.gpsimd
        def _(pool):
            pool.wait_ge(var_ready, 1)
            pool.tensor_tensor(rstd[:, :], mv[:, 1:2], wt.half[0:B, 0:1], ALU.pow).then_inc(rstd_ready, 1)

        @block.tensor
        def _(pe):
            mm, tr = nc.tensor.matmul, nc.tensor.transpose
            tr(psum[0][0:B, 0:HEADS], pcc[:, :], ident[0:HEADS, 0:HEADS]).then_inc(pe_step, 1)
            for h in range(HEADS):
                bank, lo = psum[1 + h // 8], h % 8 * DH
                for c in range(LC):
                    last = mm(bank[0:B, lo:lo + DH], xb[:, :, c * HEADS + h],
                              wt.w[:, c, VC + h * DH:VC + (h + 1) * DH], start=(c == 0), stop=(c == LC - 1))
            last.then_inc(pe_step, 1)
            pe.wait_ge(oc_ready, 1)
            for c in range(PAIRS):
                last = tr(psum[3][:, c * B:(c + 1) * B], oc[:, c * P:(c + 1) * P], ident[0:B, 0:B])
            last.then_inc(pe_step, 1)
            pe.wait_ge(ot_ready, 1)
            for c in range(PAIRS):
                last = mm(psum[4][0:B, 0:DIM], ot[:, c, :], wt.wo[:, c, :], start=(c == 0), stop=(c == PAIRS - 1))
            last.then_inc(pe_step, 1)
            pe.wait_ge(z_ready, 1)
            for c in range(LC):
                last = tr(psum[5][:, c * B:(c + 1) * B], z[:, c * P:(c + 1) * P], ident[0:B, 0:B])
            last.then_inc(pe_step, 1)
            pe.wait_ge(zt_ready, 1)
            for c in range(LC):
                last = mm(psum[6][0:M, 0:B], wt.w_in[:, c, 0:M], zt[:, c, :], start=(c == 0), stop=(c == LC - 1))
            last.then_inc(pe_step, 1)
            pe.wait_ge(g_ready, 1)
            mm(psum[7][0:B, 0:DIM], g[:, :], wt.w_out[0:M, 0, :], start=True, stop=True).then_inc(pe_step, 1)

        @block.scalar
        def _(act):
            act.wait_ge(pe_step, 6)
            nc.scalar.activation(st[:, :], psum[6][0:M, 0:B], ACT.Identity, bias=wt.b_in[0:M, 0:1]).then_inc(act_step, 1)
            act.wait_ge(act_step, 1)
            for i in range(MI):
                nc.scalar.activation(term[:, i, :], st[:, :], ACT.Relu, scale=wt.w1[0:M, i:i + 1],
                                     bias=wt.b1[0:M, i:i + 1]).then_inc(act_step, 1)

        @block.vector
        def _(dve):
            count = [0]

            def link(ins):
                count[0] += 1
                ins.then_inc(dve_step, 1)
                dve.wait_ge(dve_step, count[0])

            tt, ts = nc.vector.tensor_tensor, nc.vector.tensor_scalar
            dve.wait_ge(pe_step, 1)
            link(nc.vector.tensor_copy(pc[:, :], psum[0][0:B, 0:HEADS]))
            link(tt(oc[:, :].rearrange("b (h d) -> b h d", d=DH), wt.v_cls[0:B, :].rearrange("b (h d) -> b h d", d=DH),
                    pc[:, :].unsqueeze(2).to_broadcast([B, HEADS, DH]), ALU.mult))
            link(nc.vector.reciprocal(up[:, :], wt.unscale[0:B, 1:2]))
            dve.wait_ge(pe_step, 2)
            for j in range(2):
                link(tt(oc[:, j * 512:(j + 1) * 512], oc[:, j * 512:(j + 1) * 512], psum[1 + j][0:B, :], ALU.add))
            ts(oc[:, :], oc[:, :], up[:, 0:1], None, ALU.mult).then_inc(oc_ready, 1)
            dve.wait_ge(pe_step, 3)
            nc.vector.tensor_copy(ot[:, :, :].rearrange("p c b -> p (c b)"), psum[3][:, 0:PAIRS * B]).then_inc(ot_ready, 1)
            dve.wait_ge(pe_step, 4)
            link(tt(h1[:, :], psum[4][0:B, 0:DIM], wt.cls[0:B, :], ALU.add))
            link(nc.vector.bn_stats(bn[:, :], h1[:, :]))
            link(nc.vector.bn_aggr(mv[:, :], bn[:, :]))
            ts(mv[:, 1:2], mv[:, 1:2], LN_EPS, None, ALU.add).then_inc(var_ready, 1)
            dve.wait_ge(rstd_ready, 1)
            ts(z[:, :], h1[:, :], mv[:, 0:1], rstd[:, 0:1], ALU.subtract, ALU.mult).then_inc(z_ready, 1)
            link(tt(h1[:, :], h1[:, :], wt.b_out[0:B, :], ALU.add))
            dve.wait_ge(pe_step, 5)
            nc.vector.tensor_copy(zt[:, :, :].rearrange("p c b -> p (c b)"), psum[5][:, 0:LC * B]).then_inc(zt_ready, 1)
            dve.wait_ge(act_step, 2)
            link(ts(g[:, :], term[:, 0, :], wt.w2[0:M, 0:1], wt.b2[0:M, 0:1], ALU.mult, ALU.add))
            for i in range(1, MI):
                dve.wait_ge(act_step, i + 2)
                ins = nc.vector.scalar_tensor_tensor(g[:, :], term[:, i, :], wt.w2[0:M, i:i + 1], g[:, :], ALU.mult, ALU.add)
                if i < MI - 1:
                    link(ins)
                else:
                    ins.then_inc(g_ready, 1)
            dve.wait_ge(pe_step, 7)
            tt(y[:, :], psum[7][0:B, 0:DIM], h1[:, :], ALU.add).then_inc(y_ready, 1)



def tower(nc, x, cls_tok, log_dt, inv_a, a_imag, b_ri, ln_w, ln_b, wq, wkv, q_gamma, k_gamma, wo,
          w_in, b_in, w1, b1, w2, b2, w_out, b_out, out):
    tokens = nc.dram_tensor("tokens", (NC, SEQ, DIM), F32, kind="Internal").ap()
    ctx = ExitStack()
    with ctx:
        psum = [ctx.enter_context(nc.psum_tensor(f"bank{i}", [P, 512], F32)) for i in range(8)]
        ident = ctx.enter_context(nc.sbuf_tensor("ident", [P, P], F32))
        ident_ready = ctx.enter_context(nc.semaphore("ident_ready"))
        ident16 = ctx.enter_context(nc.sbuf_tensor("ident16", [P, P], F16))
        with nc.Block() as block:
            @block.vector
            def _(dve):
                dve.wait_ge(ident_ready, 2)
                nc.vector.tensor_copy(ident16[:, :], ident[:, :]).then_inc(ident_ready, 1)
                dve.wait_ge(ident_ready, 3)

            @block.gpsimd
            def _(pool):
                pool.memset(ident[:, :], 0.0).then_inc(ident_ready, 1)
                pool.wait_ge(ident_ready, 1)
                pool.affine_select(out=ident[:, :], in_=ident[:, :], compare_op=ALU.not_equal, fill=1.0,
                                   base=0, pattern=[[-1, P]], channel_multiplier=1).then_inc(ident_ready, 1)
                pool.wait_ge(ident_ready, 2)
        wt = Weights(nc, ctx)
        token_program(nc, psum, ident, x, log_dt, inv_a, a_imag, b_ri, tokens, wt,
                      lambda sp: load_weights(sp, wt, cls_tok, ln_w, ln_b, wq, wkv,
                                              w_in, b_in, w1, b1, w2, b2, w_out, b_out))
        wt.allocate_rest(nc, ctx)
        class_program(nc, psum, ident, wt, q_gamma, k_gamma, wo)
        pcc = ctx.enter_context(nc.sbuf_tensor("pcc", [HEADS, BATCHES], F32))
        xb = ctx.enter_context(nc.sbuf_tensor("xb", [P, BATCHES, LC * HEADS], F32))
        image_program(nc, psum, ident, ident16, wt, tokens, xb, pcc, out)
        class_rows_program(nc, psum, ident, wt, xb, pcc, out)



INPUTS = ['x', 'cls_tok', 'L0_tok_log_dt', 'L0_tok_inv_A_real', 'L0_tok_A_imag', 'L0_tok_B_ri',
          'L0_attn_ln_w', 'L0_attn_ln_b', 'L0_attn_Wq', 'L0_attn_Wkv', 'L0_attn_q_gamma', 'L0_attn_k_gamma',
          'L0_attn_Wo', 'L0_ffn_Win', 'L0_ffn_bin_', 'L0_ffn_W1', 'L0_ffn_b1', 'L0_ffn_W2', 'L0_ffn_b2',
          'L0_ffn_Wout', 'L0_ffn_bout']


def kernel(**inputs):
    import numpy as np
    import concourse.bacc as bacc
    from concourse import mybir as mb
    from concourse.bass_utils import run_bass_kernel_spmd

    nc = bacc.Bacc("TRN2", target_bir_lowering=False, num_devices=1)
    arrays, args = {}, []
    for name in INPUTS:
        a = np.ascontiguousarray(inputs[name])
        arrays[name] = a
        args.append(nc.dram_tensor(name, a.shape, mb.dt.from_np(a.dtype), kind="ExternalInput").ap())
    out = nc.dram_tensor("out", (BATCHES, SEQ + 1, DIM), mb.dt.float32, kind="ExternalOutput").ap()
    tower(nc, *args, out)
    r = run_bass_kernel_spmd(nc, [arrays], core_ids=[0])
    return r.results[0]["out"]
```
